# Optimizing a Trainium2 kernel written in Bass

```python
import numpy as np
import jax
import jax.numpy as jnp

def _softmax(x, axis=-1):
    return jax.nn.softmax(x, axis=axis)
def _gelu(x):
    return jax.nn.gelu(x, approximate=True)
def _silu(x):
    return jax.nn.silu(x)
def _sigmoid(x):
    return jax.nn.sigmoid(x)
def _layernorm(x, axis=-1, eps=1e-5):
    m = jnp.mean(x, axis=axis, keepdims=True)
    v = jnp.var(x, axis=axis, keepdims=True)
    return (x - m) / jnp.sqrt(v + eps)
def _scatter_add(tgt, idx, src, axis=0):
    return tgt.at[idx].add(src)
def _segment_sum(src, seg, n):
    return jax.ops.segment_sum(src, seg, n)

kernel_name = 'mk_conv_preact_d2_conv_nchw32_c6f2e0'

def setup_inputs(seed: int = 0):
    np.random.seed(seed)
    _w = jnp.asarray
    def _rec_inputs():
        import jax
        import jax.numpy as jnp
        _gk = jax.random.key(seed)
        x = -0.000125 + 0.9999 * jax.random.normal(jax.random.fold_in(_gk, 1), (16, 32, 256, 256), jnp.float32)
        return x
    x = _rec_inputs()
    def _L0_conv_setup():
        import jax, jax.numpy as jnp
        import numpy as np
        B, C_IN, C_OUT, H, W = (16, 32, 32, 256, 256)
        M1, M2 = (32, 32)

        def _combi_forward(x, conv_w, conv_b, w1r, w1i, w2r, w2i):
            zrow = jnp.zeros_like(x[:, :, :1, :])
            zcol = jnp.zeros_like(x[:, :, :, :1])
            dh = jnp.concatenate([x[:, :, 1:, :] - x[:, :, :-1, :], zrow], axis=2)
            dw = jnp.concatenate([x[:, :, :, 1:] - x[:, :, :, :-1], zcol], axis=3)
            feats = jnp.concatenate([x, dh, dw], axis=1)
            diff_out = jnp.einsum('bchw,oc->bohw', feats, conv_w) + conv_b[None, :, None, None]
            xf = jnp.fft.rfft2(x, axes=(-2, -1))
            w1 = w1r + 1j * w1i
            w2 = w2r + 1j * w2i
            top = jnp.einsum('bixy,ioxy->boxy', xf[:, :, :M1, :M2], w1)
            bot = jnp.einsum('bixy,ioxy->boxy', xf[:, :, -M1:, :M2], w2)
            out_ft = jnp.zeros((B, C_OUT, H, W // 2 + 1), dtype=xf.dtype)
            out_ft = out_ft.at[:, :, :M1, :M2].set(top)
            out_ft = out_ft.at[:, :, -M1:, :M2].set(bot)
            fno_out = jnp.fft.irfft2(out_ft, s=(H, W), axes=(-2, -1))
            return diff_out + fno_out
        key = jax.random.key(seed)
        ks = jax.random.split(key, 7)
        scale = 1.0 / (C_IN * C_OUT)
        return {'x': jax.random.normal(ks[0], (B, C_IN, H, W), dtype=jnp.float32), 'conv_w': jax.random.normal(ks[1], (C_OUT, 3 * C_IN), dtype=jnp.float32) * (1.0 / np.sqrt(3 * C_IN)), 'conv_b': jax.random.normal(ks[2], (C_OUT,), dtype=jnp.float32) * 0.01, 'w1r': jax.random.normal(ks[3], (C_IN, C_OUT, M1, M2), dtype=jnp.float32) * scale, 'w1i': jax.random.normal(ks[4], (C_IN, C_OUT, M1, M2), dtype=jnp.float32) * scale, 'w2r': jax.random.normal(ks[5], (C_IN, C_OUT, M1, M2), dtype=jnp.float32) * scale, 'w2i': jax.random.normal(ks[6], (C_IN, C_OUT, M1, M2), dtype=jnp.float32) * scale}
    _L0_conv_all = _L0_conv_setup()
    _L0_conv_in = {k: v for k, v in _L0_conv_all.items() if k in ('conv_w', 'conv_b', 'w1r', 'w1i', 'w2r', 'w2i', )}
    del _L0_conv_all

    def _L1_conv_setup():
        import jax, jax.numpy as jnp
        import numpy as np
        STRIDE = (1, 1)
        PADDING = (1, 1)
        key = jax.random.key(seed)
        k1, k2, k3 = jax.random.split(key, 3)
        x = jax.random.normal(k1, (8, 32, 512, 512), dtype=jnp.float32)
        weight = jax.random.uniform(k2, (32, 32, 3, 3), dtype=jnp.float32)
        bias = jax.random.uniform(k3, (32,), dtype=jnp.float32)
        return {'x': x, 'weight': weight, 'bias': bias}
    _L1_conv_all = _L1_conv_setup()
    _L1_conv_in = {k: v for k, v in _L1_conv_all.items() if k in ('weight', 'bias', )}
    del _L1_conv_all

    return {
        "x": x,
        "L0_conv_conv_w": _L0_conv_in["conv_w"],
        "L0_conv_conv_b": _L0_conv_in["conv_b"],
        "L0_conv_w1r": _L0_conv_in["w1r"],
        "L0_conv_w1i": _L0_conv_in["w1i"],
        "L0_conv_w2r": _L0_conv_in["w2r"],
        "L0_conv_w2i": _L0_conv_in["w2i"],
        "L1_conv_weight": _L1_conv_in["weight"],
        "L1_conv_bias": _L1_conv_in["bias"],
    }

def reference(x, L0_conv_conv_w, L0_conv_conv_b, L0_conv_w1r, L0_conv_w1i, L0_conv_w2r, L0_conv_w2i, L1_conv_weight, L1_conv_bias):
    import jax
    import jax.numpy as jnp
    def _L0_conv_ref(x, conv_w, conv_b, w1r, w1i, w2r, w2i):
        import jax, jax.numpy as jnp
        import numpy as np
        B, C_IN, C_OUT, H, W = (16, 32, 32, 256, 256)
        M1, M2 = (32, 32)

        def _combi_forward(x, conv_w, conv_b, w1r, w1i, w2r, w2i):
            zrow = jnp.zeros_like(x[:, :, :1, :])
            zcol = jnp.zeros_like(x[:, :, :, :1])
            dh = jnp.concatenate([x[:, :, 1:, :] - x[:, :, :-1, :], zrow], axis=2)
            dw = jnp.concatenate([x[:, :, :, 1:] - x[:, :, :, :-1], zcol], axis=3)
            feats = jnp.concatenate([x, dh, dw], axis=1)
            diff_out = jnp.einsum('bchw,oc->bohw', feats, conv_w) + conv_b[None, :, None, None]
            xf = jnp.fft.rfft2(x, axes=(-2, -1))
            w1 = w1r + 1j * w1i
            w2 = w2r + 1j * w2i
            top = jnp.einsum('bixy,ioxy->boxy', xf[:, :, :M1, :M2], w1)
            bot = jnp.einsum('bixy,ioxy->boxy', xf[:, :, -M1:, :M2], w2)
            out_ft = jnp.zeros((B, C_OUT, H, W // 2 + 1), dtype=xf.dtype)
            out_ft = out_ft.at[:, :, :M1, :M2].set(top)
            out_ft = out_ft.at[:, :, -M1:, :M2].set(bot)
            fno_out = jnp.fft.irfft2(out_ft, s=(H, W), axes=(-2, -1))
            return diff_out + fno_out
        return _combi_forward(x, conv_w, conv_b, w1r, w1i, w2r, w2i)

    def _L1_conv_ref(x, weight, bias):
        import jax, jax.numpy as jnp
        import numpy as np
        STRIDE = (1, 1)
        PADDING = (1, 1)
        out = jax.lax.conv_general_dilated(x, weight, window_strides=STRIDE, padding=[(PADDING[0], PADDING[0]), (PADDING[1], PADDING[1])], dimension_numbers=('NCHW', 'OIHW', 'NCHW'))
        out = out + bias[None, :, None, None]
        return out

    def _gn(v, G=16, eps=1e-5):
        B_, C_, H_, W_ = v.shape
        g = v.reshape(B_, G, C_ // G, H_, W_)
        m = jnp.mean(g, axis=(2, 3, 4), keepdims=True)
        s = jnp.var(g, axis=(2, 3, 4), keepdims=True)
        return ((g - m) / jnp.sqrt(s + eps)).reshape(v.shape)

    def _ln_c(v, eps=1e-6):
        m = jnp.mean(v, axis=1, keepdims=True)
        s = jnp.var(v, axis=1, keepdims=True)
        return (v - m) / jnp.sqrt(s + eps)

    def _ln_t(v, eps=1e-5):
        m = jnp.mean(v, axis=-1, keepdims=True)
        s = jnp.var(v, axis=-1, keepdims=True)
        return (v - m) / jnp.sqrt(s + eps)

    def _to_tokens(v):
        B_, C_, H_, W_ = v.shape
        return v.reshape(B_, C_, H_ * W_).transpose(0, 2, 1)
    def _from_tokens(t, like):
        B_, C_, H_, W_ = like.shape
        return t.transpose(0, 2, 1).reshape(B_, C_, H_, W_)

    x = x + _L0_conv_ref(_gn(x), L0_conv_conv_w, L0_conv_conv_b, L0_conv_w1r, L0_conv_w1i, L0_conv_w2r, L0_conv_w2i)
    x = x + _L1_conv_ref(_gn(x), L1_conv_weight, L1_conv_bias)
    return x


_drawn_inputs = setup_inputs


def setup_inputs(seed=0):
    import zlib

    import numpy as np

    out = dict(_drawn_inputs(seed))
    spreads = {}
    factors = {'L0_conv_conv_b': 8.0,
     'L0_conv_w1r': 33.582,
     'L0_conv_w1i': 33.396,
     'L0_conv_w2r': 33.763,
     'L0_conv_w2i': 33.734}
    for name, (base, spread) in spreads.items():
        noise = np.random.default_rng([zlib.crc32(name.encode()), seed]).standard_normal(out[name].shape)
        drawn = base * np.exp(spread * noise) if base else spread * noise
        out[name] = jnp.asarray(drawn.astype(out[name].dtype))
    for name, factor in factors.items():
        out[name] = (out[name] * factor).astype(out[name].dtype)
    return out
```

```python
from contextlib import ExitStack

import numpy as np

import concourse.bass as bass
from concourse import mybir

F32 = mybir.dt.float32
F16 = mybir.dt.float16
ALU = mybir.AluOpType
ACT = mybir.ActivationFunctionType
AX_X = mybir.AxisListType.X

B, C, H, W = 16, 32, 256, 256
M1, M2 = 32, 32
P = 128
EPS = 1e-5

CC = 8
NQ = C // CC
NG = CC // 2
NK = M1 + 1
KS = 4
KP = -(-NK // KS) * KS
KQ = KP // KS
ND = 4 * KS

TQ = 4
NT = M1 // TQ
MJ = 4
MM = M2 // MJ

J = 4
GC = 4
NC = H // (J * GC)
RING = 4
GR = RING * GC
WP = W + 4
X0 = 2
NP = 3
NQD = NC // RING
IP = 4
PER = NC + IP + NC


def tables():
    def split(a):
        hi = a.astype(np.float16)
        return hi, (a - hi.astype(np.float64)).astype(np.float16)

    n = np.arange(256)
    ang = 2 * np.pi / 256
    fwd_h = np.concatenate([np.cos(ang * np.outer(n, np.arange(NK))), np.sin(ang * np.outer(n, np.arange(NK)))], 1)
    fwd_h = fwd_h.reshape(2, P, 2 * NK).transpose(1, 0, 2)
    th = np.stack(split(fwd_h), 1)
    phi = ang * np.outer(n, np.arange(M2))
    c, s = np.cos(phi), np.sin(phi)
    of_cos = np.stack([np.stack([c, -s], 1)] * 2, 1)
    of_sin = np.stack([np.stack([-s, -c], 1), np.stack([s, c], 1)], 1)
    fwd_w = np.stack([of_cos, of_sin]).reshape(2, 2, P, 4 * M2).transpose(2, 0, 1, 3)
    tw = np.stack(split(fwd_w), 1)
    kx = np.concatenate([np.arange(M1), -1 - np.arange(M1)])
    the = ang * np.outer(kx, n)
    inv_h = np.stack([np.concatenate([np.cos(the), -np.sin(the)]),
                      np.concatenate([np.sin(the), np.cos(the)])], 1) / (H * W)
    amp = np.where(np.arange(M2) == 0, 1.0, 2.0)[:, None]
    inv_w = np.concatenate([amp * np.cos(phi.T), -amp * np.sin(phi.T)])
    iw = np.stack(split(np.concatenate([inv_w, inv_w])), 1)
    ch = np.arange(P) % C
    mean_of_group = (ch[:, None] // 2 == ch[None, :] // 2) / (2.0 * J)
    mats = np.stack([mean_of_group, np.full((P, P), 1.0 / P), np.eye(P)], 1)
    return {"t_fwd_h": np.ascontiguousarray(th), "t_fwd_w": np.ascontiguousarray(tw),
            "t_inv_h": inv_h.astype(np.float32), "t_inv_w": np.ascontiguousarray(iw),
            "t_mats": mats.astype(np.float32)}


def wait(eng, sem, count):
    if not (isinstance(count, int) and count <= 0):
        eng.wait_ge(sem, count)


def program(nc, x, cw, cb, w1r, w1i, w2r, w2i, w3, b3, t_fwd_h, t_fwd_w, t_inv_h, t_inv_w, t_mats, out):
    stat_d = nc.dram_tensor("stat_scratch", [B, 2, C], F32).ap()
    modes_d = nc.dram_tensor("modes_scratch", [B, P, M2 * C], F32).ap()
    with ExitStack() as ctx:
        gmax = ctx.enter_context(nc.sbuf_tensor("gmax", [P, 1], F32))
        mats = ctx.enter_context(nc.sbuf_tensor("mats", [P, 3, P], F32))
        with ExitStack() as both:
            modes = both.enter_context(nc.sbuf_tensor("modes", [P, B, M1, M2], F32))
            spectra(nc, x, t_fwd_h, t_fwd_w, t_mats, mats, modes, stat_d)
            mixing(nc, w1r, w1i, w2r, w2i, modes, modes_d, gmax)
        images(nc, x, cw, cb, w3, b3, t_inv_h, t_inv_w, mats, gmax, stat_d, modes_d, out)


def spectra(nc, x, t_fwd_h, t_fwd_w, t_mats, mats, modes, stat_d):
    N = B * NQ
    with ExitStack() as ctx:
        def sb(name, shape, dt):
            return ctx.enter_context(nc.sbuf_tensor(f"sp_{name}", shape, dt))

        def sem(name):
            return ctx.enter_context(nc.semaphore(f"sp_{name}"))

        xt = [sb(f"xt{i}", [P, CC, 2, W], F32) for i in range(NQ)]
        hi = [sb(f"hi{i}", [P, CC, 2, W], F16) for i in range(2)]
        lo = [sb(f"lo{i}", [P, CC, 2, W], F16) for i in range(2)]
        th = sb("th", [P, 2, 2, 2 * NK], F16)
        tw = sb("tw", [P, 2, 2, 2, 4 * M2], F16)
        y = sb("y", [P, 2, 2, 2, KP, C], F16)
        xi = sb("xi", [P, KQ, 2, 2, M2], F32)
        st = sb("st", [P, CC, 6], F32)
        mv = sb("mv", [P, NG, 2], F32)
        pad = sb("pad", [P, 1], F32)
        dm = sb("dm", [P, NG], F32)
        sq = sb("sq", [P, NG], F32)
        vv = sb("vv", [P, NG], F32)
        sd = sb("sd", [P, NG], F32)
        eps = sb("eps", [P, 1], F32)
        sn = sb("sn", [P, 2, NQ, NG], F32)
        ps_y = [ctx.enter_context(nc.psum_tensor(f"ps_y{i}", [P, 512], F32)) for i in range(4)]
        ps_x = ctx.enter_context(nc.psum_tensor("ps_x", [P, 3, 512], F32))
        ps_s = ctx.enter_context(nc.psum_tensor("ps_s", [P, 2, 256], F32))

        tables_in = sem("tables_in")
        x_in = [sem(f"x_in{i}") for i in range(NQ)]
        ready = sem("ready")
        own = sem("own_chain")
        stats_in = sem("stats_in")
        stats_out = sem("stats_out")
        std_out = sem("std_out")
        norm_out = sem("norm_out")
        h_out = sem("h_out")
        hi_out = sem("hi_out")
        lo_out = sem("lo_out")
        y_ps = sem("y_ps")
        y_hi = sem("y_hi")
        y_lo = sem("y_lo")
        x_ps = sem("x_ps")
        x_sb = sem("x_sb")
        moved = sem("moved")
        stat_st = sem("stat_st")
        block = ctx.enter_context(nc.Block())

        @block.sync
        def _(sp):
            sp.dma_start(th[:], t_fwd_h).then_inc(tables_in, 16)
            sp.dma_start(tw[:], t_fwd_w).then_inc(tables_in, 16)
            sp.dma_start(mats[:], t_mats).then_inc(tables_in, 16)

            def load(b, q):
                for hh in range(2):
                    sp.dma_start(xt[q][:, :, hh, :],
                                 x[b, CC * q:CC * (q + 1), hh * P:(hh + 1) * P, :].rearrange("c h w -> h c w")
                                 ).then_inc(x_in[q], 16)

            def keep_stats(b):
                sp.wait_ge(norm_out, NQ * b + NQ)
                with nc.allow_non_contiguous_dma("a few words"):
                    for r in range(2):
                        for t in range(2):
                            sp.dma_start(stat_d[bass.ds(b, 1), t].rearrange("u (g r) -> r u g", r=2)[r],
                                         sn[0:1, t].rearrange("u q g -> u (q g)")).then_inc(stat_st, 16)

            def place(b):
                sp.wait_ge(x_sb, b + 1)
                for kk in range(KS):
                    for ri in range(2):
                        sp.dma_start(modes[32 * ri:32 * ri + 32, b, kk:M1:KS, :],
                                     xi[32 * kk:32 * kk + 32, 0:M1 // KS, 0, ri, :]).then_inc(moved, 16)
                        q0 = int(kk == 0)
                        k0 = KS * q0 + kk - 1
                        sp.dma_start(modes[64 + 32 * ri:96 + 32 * ri, b, k0:M1:KS, :],
                                     xi[32 * kk:32 * kk + 32, q0:q0 + M1 // KS, 1, ri, :]).then_inc(moved, 16)

            for q in range(NQ):
                load(0, q)
            with sp.Fori(0, B - 1) as b:
                for q in range(NQ):
                    sp.wait_ge(lo_out, NQ * b + q + 1)
                    load(b + 1, q)
                    if q == 1:
                        keep_stats(b)
                place(b)
            keep_stats(B - 1)
            place(B - 1)
            sp.wait_ge(moved, 16 * ND * B)
            sp.wait_ge(stat_st, 64 * B)

        @block.gpsimd
        def _(pool):
            def step(n, q):
                pool.wait_ge(hi_out, n + 1)
                wait(pool, y_ps, 4 * (n - 1))
                nc.gpsimd.tensor_tensor(lo[q % 2][:], xt[q][:], hi[q % 2][:], ALU.subtract).then_inc(lo_out, 1)

            for q in range(NQ):
                step(q, q)
            with pool.Fori(1, B) as b:
                for q in range(NQ):
                    step(NQ * b + q, q)

        @block.scalar
        def _(act):
            act.wait_ge(ready, 2)

            def normalise(n, q):
                act.wait_ge(stats_out, 2 * n + 2)
                nc.scalar.activation(sd[:], ps_s[:, 1, 0:NG], ACT.Sqrt, bias=eps[:, 0:1]).then_inc(std_out, 1)
                act.wait_ge(norm_out, n + 1)
                for g in range(NG):
                    v = xt[q][:, 2 * g:2 * g + 2, :, :].rearrange("p c a w -> p (c a w)")
                    last = nc.scalar.activation(v, v, ACT.Identity, bias=sn[:, 1, q, g:g + 1], scale=sn[:, 0, q, g:g + 1])
                last.then_inc(h_out, 1)

            def y_high(n, q):
                for i in range(4):
                    act.wait_ge(y_ps, 4 * n + i + 1)
                    ch, wh = i // 2, i % 2
                    c0 = CC * q + 4 * ch
                    nc.scalar.copy(y[:, 0, wh, :, 0:NK, c0:c0 + 4].rearrange("p s k c -> p c s k"),
                                   ps_y[i][:, 0:8 * NK].rearrange("p (c s k) -> p c s k", c=4, s=2)).then_inc(y_hi, 1)

            def modes_out(b):
                act.wait_ge(x_ps, b + 1)
                wait(act, moved, 16 * ND * b)
                for i in range(3):
                    w = min(4, KQ - 4 * i)
                    last = nc.scalar.copy(xi[:, 4 * i:4 * i + w].rearrange("p q s r k -> p (q s r k)"),
                                          ps_x[:, i, 0:w * P])
                last.then_inc(x_sb, 1)

            def step(b, q, ahead=True):
                if ahead:
                    normalise(NQ * b + q + 2, (q + 2) % NQ)
                y_high(NQ * b + q, q)
                if q == NQ - 1:
                    modes_out(b)

            normalise(0, 0)
            normalise(1, 1)
            for q in range(NQ):
                step(0, q)
            with act.Fori(1, B - 1) as b:
                for q in range(NQ):
                    step(b, q)
            for q in range(NQ):
                step(B - 1, q, ahead=q < 2)

        LINKS = 4

        @block.vector
        def _(dve):
            nc.vector.memset(eps[:], EPS).then_inc(ready, 1)
            nc.vector.memset(y[:, :, :, :, NK:KP, :].rearrange("p a b c k d -> p (a b c) (k d)"), 0.0).then_inc(ready, 1)
            dve.wait_ge(ready, 2)

            def chain(b, q):
                n = NQ * b + q
                m = LINKS * n
                dve.wait_ge(x_in[q], 32 * b + 32)
                for c in range(CC):
                    last = nc.vector.bn_stats(st[:, c, :], xt[q][:, c].rearrange("p a w -> p (a w)"))
                last.then_inc(own, 1)
                dve.wait_ge(own, m + 1)
                nc.vector.tensor_copy(pad[:], st[:, 0, 0:1])
                for g in range(NG):
                    last = nc.vector.bn_aggr(mv[:, g, :], st[:, 2 * g:2 * g + 2, :].rearrange("p a b -> p (a b)"))
                last.then_inc(stats_in, 1)
                dve.wait_ge(stats_in, 2 * n + 1)
                dve.wait_ge(stats_out, 2 * n + 1)
                nc.vector.tensor_tensor(dm[:], mv[:, :, 0], ps_s[:, 0, 0:NG], ALU.subtract).then_inc(own, 1)
                dve.wait_ge(own, m + 2)
                nc.vector.tensor_tensor(sq[:], dm[:], dm[:], ALU.mult).then_inc(own, 1)
                dve.wait_ge(own, m + 3)
                nc.vector.tensor_tensor(vv[:], sq[:], mv[:, :, 1], ALU.add).then_inc(stats_in, 1)
                dve.wait_ge(std_out, n + 1)
                if q == 0:
                    wait(dve, stat_st, 64 * b)
                nc.vector.reciprocal(sn[:, 0, q, :], sd[:]).then_inc(own, 1)
                dve.wait_ge(own, m + 4)
                nc.vector.scalar_tensor_tensor(out=sn[:, 1, q, :], in0=ps_s[:, 0, 0:NG], scalar=-1.0,
                                               in1=sn[:, 0, q, :], op0=ALU.mult, op1=ALU.mult).then_inc(norm_out, 1)

            def high(n, q):
                dve.wait_ge(h_out, n + 1)
                wait(dve, y_ps, 4 * (n - 1))
                nc.vector.tensor_copy(hi[q % 2][:], xt[q][:]).then_inc(hi_out, 1)

            def y_low(n, q):
                for i in range(4):
                    dve.wait_ge(y_hi, 4 * n + i + 1)
                    ch, wh = i // 2, i % 2
                    c0 = CC * q + 4 * ch
                    nc.vector.tensor_tensor(
                        y[:, 1, wh, :, 0:NK, c0:c0 + 4].rearrange("p s k c -> p c s k"),
                        ps_y[i][:, 0:8 * NK].rearrange("p (c s k) -> p c s k", c=4, s=2),
                        y[:, 0, wh, :, 0:NK, c0:c0 + 4].rearrange("p s k c -> p c s k"), ALU.subtract).then_inc(y_lo, 1)

            def step(b, q, far=True, near=True):
                n = NQ * b + q
                if near:
                    high(n + 1, (q + 1) % NQ)
                if far:
                    chain(b + (q + 2) // NQ, (q + 2) % NQ)
                y_low(n, q)

            chain(0, 0)
            high(0, 0)
            chain(0, 1)
            for q in range(NQ):
                step(0, q)
            with dve.Fori(1, B - 1) as b:
                for q in range(NQ):
                    step(b, q)
            for q in range(NQ):
                step(B - 1, q, far=q < 2, near=q < 3)

        @block.tensor
        def _(pe):
            pe.wait_ge(tables_in, 48)
            pe.wait_ge(ready, 2)

            def means(n):
                pe.wait_ge(stats_in, 2 * n + 1)
                nc.tensor.matmul(ps_s[:, 0, 0:NG], mats[:, 1, :], mv[:, :, 0], start=True, stop=True).then_inc(stats_out, 1)
                pe.wait_ge(stats_in, 2 * n + 2)
                nc.tensor.matmul(ps_s[:, 1, 0:NG], mats[:, 1, :], vv[:], start=True, stop=True).then_inc(stats_out, 1)

            def along_h(n, q):
                pe.wait_ge(lo_out, n + 1)
                wait(pe, y_lo, 4 * n)
                for i in range(4):
                    ch, wh = i // 2, i % 2
                    for c in range(4):
                        o = ps_y[i][:, 2 * NK * c:2 * NK * (c + 1)]
                        k = 0
                        for hh in range(2):
                            for part, hl in ((hi, 0), (hi, 1), (lo, 0)):
                                last = nc.tensor.matmul(
                                    o, part[q % 2][:, 4 * ch + c, hh, wh * P:(wh + 1) * P], th[:, hl, hh, :],
                                    start=(k == 0), stop=(k == 5))
                                k += 1
                    last.then_inc(y_ps, 1)

            def along_w(b):
                pe.wait_ge(y_lo, 4 * NQ * b + 4 * NQ)
                wait(pe, x_sb, b)
                for kq in range(KQ):
                    k = 0
                    for cs in range(2):
                        for wh in range(2):
                            for yl, tl in ((0, 0), (0, 1), (1, 0)):
                                last = nc.tensor.matmul(
                                    ps_x[:, kq // 4, (kq % 4) * P:(kq % 4 + 1) * P],
                                    y[:, yl, wh, cs, KS * kq:KS * (kq + 1), :].rearrange("p k c -> p (k c)"),
                                    tw[:, tl, cs, wh, :], start=(k == 0), stop=(k == 11))
                                k += 1
                last.then_inc(x_ps, 1)

            def step(b, q, ahead=True):
                n = NQ * b + q
                if ahead:
                    means(n + 2)
                along_h(n, q)
                if q == NQ - 1:
                    along_w(b)

            means(0)
            means(1)
            for q in range(NQ):
                step(0, q)
            with pe.Fori(1, B - 1) as b:
                for q in range(NQ):
                    step(b, q)
            for q in range(NQ):
                step(B - 1, q, ahead=q < 2)


def mixing(nc, w1r, w1i, w2r, w2i, modes, modes_d, gmax):
    with ExitStack() as ctx:
        def sb(name, shape, dt):
            return ctx.enter_context(nc.sbuf_tensor(f"mx_{name}", shape, dt))

        def sem(name):
            return ctx.enter_context(nc.semaphore(f"mx_{name}"))

        w = [sb(f"w{i}", [P, C, TQ, M2], F32) for i in range(2)]
        xx = [sb(f"xx{i}", [P, M2, 2, B], F32) for i in range(2)]
        g = [sb(f"g{i}", [P, 2, TQ, MM * C], F32) for i in range(2)]
        top = sb("top", [P, 1], F32)
        ps = [[ctx.enter_context(nc.psum_tensor(f"ps_m{i}{t}", [P, 512], F32)) for t in range(2)] for i in range(4)]

        w_in = [sem(f"w_in{i}") for i in range(2)]
        xx_a = sem("xx_a")
        xx_d = sem("xx_d")
        mixed = sem("mixed")
        g_out = sem("g_out")
        max_own = sem("max_own")
        g_st = [sem(f"g_st{i}") for i in range(2)]
        STORES = 16 * 2 * MJ * 2
        block = ctx.enter_context(nc.Block())

        def fill(copy, negate, dst, t, s):
            r, i = slice(64 * s, 64 * s + 32), slice(64 * s + 32, 64 * s + 64)

            def src(part):
                return modes[part, :, t, :].rearrange("p b k -> p k b")

            copy(dst[r, :, 0, :], src(r))
            copy(dst[r, :, 1, :], src(i))
            copy(dst[i, :, 1, :], src(r))
            return negate(dst[i, :, 0, :], src(i))

        @block.sync
        def _(sp):
            def load(k, slot):
                for part, src, t0 in ((0, w1r, TQ * k), (1, w1i, TQ * k),
                                      (2, w2r, M1 - TQ - TQ * k), (3, w2i, M1 - TQ - TQ * k)):
                    sp.dma_start(w[slot][32 * part:32 * part + 32], src[:, :, bass.ds(t0, TQ), :]).then_inc(w_in[slot], 16)

            def store(k, slot):
                sp.wait_ge(g_out, TQ * k + TQ)
                for s in range(2):
                    for j in range(MJ):
                        for ri in range(2):
                            p0 = 32 * j + 16 * ri
                            sp.dma_start(
                                modes_d[:, bass.ds(64 * ri + 32 * s + TQ * k, TQ), MM * C * j:MM * C * (j + 1)],
                                g[slot][p0:p0 + B, s]).then_inc(g_st[slot], 16)

            load(0, 0)
            load(1, 1)
            with sp.Fori(0, NT // 2 - 1) as h:
                for slot in range(2):
                    sp.wait_ge(mixed, TQ * (2 * h + slot + 1))
                    load(2 * h + slot + 2, slot)
                    store(2 * h + slot, slot)
            for slot in range(2):
                store(NT - 2 + slot, slot)
            for slot in range(2):
                sp.wait_ge(g_st[slot], STORES * (NT // 2))

        def each_step(eng, body):
            for slot in range(2):
                body(0, slot)
            with eng.Fori(1, NT // 2) as h:
                for slot in range(2):
                    body(h, slot)

        @block.scalar
        def _(act):
            def evacuate(h, slot, t):
                k = 2 * h + slot
                act.wait_ge(mixed, TQ * k + t + 1)
                if t == 0:
                    wait(act, max_own, 2 * (k - 1))
                    wait(act, g_st[slot], STORES * h)
                for s in range(2):
                    last = nc.scalar.copy(g[slot][:, s, t, :], ps[t][s][:, 0:MM * C])
                last.then_inc(g_out, 1)

            def body(h, slot):
                for t in range(TQ):
                    n = TQ * (2 * h + slot) + t
                    wait(act, mixed, n - 1)
                    fill(nc.scalar.copy, lambda o, a: nc.scalar.mul(o, a, -1.0), xx[t % 2], n, 1).then_inc(xx_a, 1)
                    if t:
                        evacuate(h, slot, t - 1)
                evacuate(h, slot, TQ - 1)

            each_step(act, body)

        @block.vector
        def _(dve):
            def largest(k, slot):
                dve.wait_ge(g_out, TQ * k + TQ)
                dve.wait_ge(max_own, 2 * k + 1)
                nc.vector.tensor_reduce(top[:], g[slot][:].rearrange("p s t k -> p (s t k)"), AX_X, ALU.max,
                                        apply_absolute_value=True).then_inc(max_own, 1)
                dve.wait_ge(max_own, 2 * k + 2)
                nc.vector.tensor_tensor(gmax[:], gmax[:], top[:], ALU.max).then_inc(max_own, 1)

            def body(h, slot):
                k = 2 * h + slot
                for t in range(TQ):
                    n = TQ * k + t
                    wait(dve, mixed, n - 1)
                    fill(nc.vector.tensor_copy,
                         lambda o, a: nc.vector.tensor_scalar(o, a, -1.0, None, ALU.mult), xx[t % 2], n, 0
                         ).then_inc(xx_d, 1)
                if not (isinstance(k, int) and k == 0):
                    largest(k - 1, 1 - slot)

            nc.vector.memset(gmax[:], 0.0).then_inc(max_own, 1)
            each_step(dve, body)
            largest(NT - 1, 1)
            dve.wait_ge(max_own, 2 * NT + 1)

        @block.tensor
        def _(pe):
            def body(h, slot):
                pe.wait_ge(w_in[slot], 64 * h + 64)
                for t in range(TQ):
                    n = TQ * (2 * h + slot) + t
                    pe.wait_ge(xx_d, n + 1)
                    pe.wait_ge(xx_a, n + 1)
                    wait(pe, g_out, n - TQ + 1)
                    nc.tensor.matmul(ps[t][0][0:32, 511:512], xx[t % 2][:, 0].rearrange("p r b -> p (r b)"),
                                     xx[t % 2][:, 0, 0, 0:1], start=True, stop=True)
                    for m in range(MM):
                        for s in range(2):
                            rows = slice(64 * s, 64 * s + 64)
                            for j in range(MJ):
                                ky = MM * j + m
                                last = nc.tensor.matmul(
                                    ps[t][s][32 * j:32 * j + 32, C * m:C * (m + 1)],
                                    xx[t % 2][rows, ky].rearrange("p r b -> p (r b)"),
                                    w[slot][rows, :, TQ - 1 - t if s else t, ky], start=True, stop=True)
                    last.then_inc(mixed, 1)

            each_step(pe, body)


def images(nc, x, cw, cb, w3, b3, t_inv_h, t_inv_w, mats, gmax, stat_d, modes_d, out):
    with ExitStack() as ctx:
        def sb(name, shape, dt):
            return ctx.enter_context(nc.sbuf_tensor(f"im_{name}", shape, dt))

        def sem(name):
            return ctx.enter_context(nc.semaphore(f"im_{name}"))

        win = [sb(f"win{a}", [P, 2, GR, WP], F16) for a in range(2)]
        mid = [sb(f"mid{a}", [P, 2, GR, WP], F16) for a in range(2)]
        x1 = sb("x1", [P, H // J, W], F32)
        xb = [sb(f"xb{i}", [P, GC, W], F32) for i in range(RING)]
        hn = [sb(f"hn{i}", [P, GC, W + 1], F32) for i in range(2)]
        ob = [sb(f"ob{i}", [P, GC, W], F32) for i in range(2)]
        gi = sb("gi", [P, H, C], F16)
        gm = sb("gm", [P, M2, C], F32)
        ih = sb("ih", [P, 2, H], F32)
        iw = sb("iw", [P, 2, W], F16)
        lw0 = sb("lw0", [P, 2, 2, 2, C], F16)
        lw1 = sb("lw1", [P, 2, 2, 3, C], F16)
        bs = sb("bs", [P, 2 * NC, 6], F32)
        sc0 = sb("sc0", [P, B, 2], F32)
        scc = sb("scc", [P, 2], F32)
        sc1 = sb("sc1", [P, 2], F32)
        mv = sb("mv", [P, 2], F32)
        mc = sb("mc", [P, 1], F32)
        pad = sb("pad", [P, 1], F32)
        dm = sb("dm", [P, 1], F32)
        vv = sb("vv", [P, 1], F32)
        sd = sb("sd", [P, 1], F32)
        ns = sb("ns", [P, 1], F32)
        eps = sb("eps", [P, 1], F32)
        b3p = sb("b3p", [P, 1], F32)
        dc = sb("dc", [1, C], F32)
        q = sb("q", [P, 4], F32)
        ps = ctx.enter_context(nc.psum_tensor("ps", [P, 2 * NP, 512], F32))
        ps_s = ctx.enter_context(nc.psum_tensor("ps_s3", [P, 512], F32))

        setup(nc, cw, cb, w3, b3, t_inv_h, t_inv_w, mats, gmax, stat_d, win, mid, ih, iw, lw0, lw1,
              sc0, eps, b3p, dc, q, ps_s)

        x_in = [sem(f"xb_in{i}") for i in range(RING)]
        h_out = sem("hn_out")
        hi_out = sem("win_hi")
        lo_out = sem("win_lo")
        mid_in = [[sem(f"mid_in{a}{i}") for i in range(RING)] for a in range(2)]
        below = [sem("below0"), sem("below1")]
        above = sem("above1")
        conv = [sem("conv0"), sem("conv1")]
        inv_ps = sem("inv_ps")
        inv_hi = sem("inv_hi")
        inv_lo = sem("inv_lo")
        bn_out = sem("bn_out")
        x1_out = sem("x1_out")
        o_out = sem("o_out")
        o_st = [sem(f"o_st{i}") for i in range(2)]
        gm_in = sem("gm_in")
        gm_dc = sem("gm_dc")
        own = sem("own3")
        mean_in = sem("mean_in")
        mean_out = sem("mean_out")
        scc_out = sem("scc_out")
        std_out = sem("std3_out")
        norm_out = sem("norm3_out")
        block = ctx.enter_context(nc.Block())

        def copies(a, slot):
            g0 = GC * slot
            r = [(mid[a][64:128, :, g0:g0 + GC, :], win[a][0:64, :, g0:g0 + GC, :])]
            if slot < RING - 1:
                r.append((mid[a][0:64, :, g0 + 1:g0 + GC + 1, :], win[a][64:128, :, g0:g0 + GC, :]))
            else:
                r.append((mid[a][0:64, :, g0 + 1:GR, :], win[a][64:128, :, g0:GR - 1, :]))
                r.append((mid[a][0:64, :, 0:1, :], win[a][64:128, :, GR - 1:GR, :]))
            return r

        def mid_count(a, b, kq, slot):
            return 16 * len(copies(a, slot)) * (NC // RING * b + kq + 1)

        zeros = sb("zeros", [P, 2, 1, WP], F16)
        zeroed = sem("zeroed")

        def peeled(eng, body):
            body(0)
            with eng.Fori(1, B - 1) as b:
                body(b)
            body(B - 1, last=True)

        @block.sync
        def _(sp):
            def load(b, k, slot):
                n = NC * b + k
                wait(sp, x1_out, n - RING + 1)
                for j in range(J):
                    sp.dma_start(xb[slot][32 * j:32 * j + 32],
                                 x[b].rearrange("c (k g j) w -> j c k g w", j=J, g=GC)[j, :, k]
                                 ).then_inc(x_in[slot], 16)

            def shift(a, b, kq, slot):
                sp.wait_ge(lo_out, 2 * NC * b + NC * a + RING * kq + slot + 1)
                for dst, src in copies(a, slot):
                    sp.dma_start(dst, src).then_inc(mid_in[a][slot], 16)

            def store(b, k, slot):
                sp.wait_ge(zeroed, 1)
                sp.wait_ge(o_out, NC * b + k + 1)
                for j in range(J):
                    sp.dma_start(out[b].rearrange("c (k g j) w -> j c k g w", j=J, g=GC)[j, :, k],
                                 ob[slot % 2][32 * j:32 * j + 32]).then_inc(o_st[slot % 2], 16)

            def body(b, last=False):
                if not last:
                    wait(sp, inv_ps, IP * (b + 1))
                    sp.dma_start(gm[:], modes_d[b + 1].rearrange("p (k o) -> p k o", k=M2)).then_inc(gm_in, 16)
                for slot in range(RING):
                    shift(0, b, 0, slot)
                    if slot >= 2:
                        load(b, slot + 2, slot - 2)
                with sp.Fori(1, NQD - 1) as kq:
                    for slot in range(RING):
                        shift(0, b, kq, slot)
                        load(b, RING * kq + slot + 2, (slot + 2) % RING)
                for slot in range(RING):
                    shift(0, b, NQD - 1, slot)
                    if slot < 2:
                        load(b, NC - RING + slot + 2, slot + 2)
                sp.wait_ge(conv[0], 2 * NC * b + 2 * (NC - RING + 1))
                for r0 in (64, 96):
                    sp.dma_start(mid[0][r0:r0 + 32, :, 0:1, :], win[0][96:128, :, GR - 1:GR, :]).then_inc(below[0], 16)
                if not last:
                    for slot in range(RING):
                        load(b + 1, slot, slot)
                wait(sp, conv[1], 2 * NC * b)
                sp.dma_start(mid[1][0:64, :, 0:1, :], zeros[0:64]).then_inc(above, 16)
                for slot in range(RING):
                    shift(1, b, 0, slot)
                    if slot == 3:
                        store(b, 0, 0)
                with sp.Fori(1, NQD) as kq:
                    for slot in range(RING):
                        shift(1, b, kq, slot)
                        store(b, RING * kq + slot - 3, slot + 1)
                sp.dma_start(mid[1][64:128, :, 0:1, :], zeros[64:128]).then_inc(below[1], 16)
                for k in range(NC - 3, NC):
                    store(b, k, k)

            sp.wait_ge(zeroed, 1)
            sp.dma_start(gm[:], modes_d[0].rearrange("p (k o) -> p k o", k=M2)).then_inc(gm_in, 16)
            for slot in range(RING):
                load(0, slot, slot)
            peeled(sp, body)
            for i in range(2):
                sp.wait_ge(o_st[i], 16 * J * B * NC // 2)

        @block.gpsimd
        def _(pool):
            nc.gpsimd.memset(zeros[:], 0.0).then_inc(zeroed, 1)

            def body(b, last=False):
                for n in range(2 * NC):
                    a, k = divmod(n, NC)
                    g0 = GC * k % GR
                    pool.wait_ge(hi_out, 2 * NC * b + n + 1)
                    nc.gpsimd.tensor_tensor(win[a][:, 1, g0:g0 + GC, X0:X0 + W + 1 - a], hn[n % 2][:, :, 0:W + 1 - a],
                                            win[a][:, 0, g0:g0 + GC, X0:X0 + W + 1 - a], ALU.subtract
                                            ).then_inc(lo_out, 1)

            peeled(pool, body)

        @block.scalar
        def _(act):
            def produce(a, b, k):
                n = 2 * NC * b + NC * a + k
                g0 = GC * k % GR
                wait(act, lo_out, n - 1)
                wait(act, conv[a], 2 * NC * b + max(0, 2 * (k - 2)))
                wd = W + 1 - a
                if a == 0:
                    act.wait_ge(x_in[k % RING], 16 * J * ((NC // RING) * b + k // RING + 1))
                    s, t = scc[:, 0:1], scc[:, 1:2]
                    nc.scalar.activation(hn[k % 2][:, :, 0:W], xb[k % RING][:], ACT.Identity, bias=t, scale=s).then_inc(h_out, 1)
                    nc.scalar.activation(hn[k % 2][:, :, W:W + 1], xb[k % RING][:, :, W - 1:W], ACT.Identity,
                                         bias=t, scale=s).then_inc(h_out, 1)
                    act.wait_ge(h_out, 3 * NC * b + 2 * k + 2)
                else:
                    nc.scalar.activation(hn[k % 2][:, :, 0:W], x1[:, GC * k:GC * (k + 1)], ACT.Identity,
                                         bias=sc1[:, 1:2], scale=sc1[:, 0:1]).then_inc(h_out, 1)
                    act.wait_ge(h_out, 3 * NC * b + 2 * NC + k + 1)
                nc.scalar.copy(win[a][:, 0, g0:g0 + GC, X0:X0 + wd], hn[k % 2][:, :, 0:wd]).then_inc(hi_out, 1)

            def invert(b, i, slot):
                act.wait_ge(inv_ps, IP * b + i + 1)
                for h in range(2):
                    last = nc.scalar.copy(
                        gi[0:64, :, 8 * i + h:8 * i + 8:2].rearrange("p h o -> p o h"),
                        ps[64 * h:64 * h + 64, 2 * slot:2 * slot + 2].rearrange("p a (c h) -> p (a c) h", c=2))
                last.then_inc(inv_hi, 1)

            def body(b, last=False):
                nc.scalar.copy(scc[:], sc0[:, b:b + 1, :] if isinstance(b, int) else sc0[:, bass.ds(b, 1), :]).then_inc(scc_out, 1)
                act.wait_ge(scc_out, b + 1)
                for k in range(NC):
                    produce(0, b, k)
                act.wait_ge(mean_out, 2 * b + 2)
                nc.scalar.activation(sd[:], ps_s[:, 1:2], ACT.Sqrt, bias=eps[:, 0:1]).then_inc(std_out, 1)
                if not last:
                    for i in range(IP):
                        invert(b + 1, i, (IP + NC + i) % NP)
                act.wait_ge(norm_out, b + 1)
                for k in range(NC):
                    produce(1, b, k)

            for i in range(IP):
                invert(0, i, i % NP)
            peeled(act, body)

        LINKS = 5

        @block.vector
        def _(dve):
            def invert(b, i, slot):
                dve.wait_ge(inv_hi, IP * b + i + 1)
                for h in range(2):
                    last = nc.vector.tensor_tensor(
                        gi[64:128, :, 8 * i + h:8 * i + 8:2].rearrange("p h o -> p o h"),
                        ps[64 * h:64 * h + 64, 2 * slot:2 * slot + 2].rearrange("p a (c h) -> p (a c) h", c=2),
                        gi[0:64, :, 8 * i + h:8 * i + 8:2].rearrange("p h o -> p o h"), ALU.subtract)
                last.then_inc(inv_lo, 1)

            def constant_mode(b):
                dve.wait_ge(gm_in, 16 * b + 16)
                nc.vector.tensor_tensor(gm[0:1, 0, :], gm[0:1, 0, :], dc[:], ALU.add).then_inc(gm_dc, 1)

            def evacuate(a, b, k):
                i = IP + (NC + IP) * a + k
                slot = i % NP
                dve.wait_ge(conv[a], 2 * NC * b + 2 * k + 2)
                banks = ps[:, 2 * slot:2 * slot + 2, :].rearrange("p a w -> p (a w)")
                if a == 0:
                    nc.vector.scalar_tensor_tensor(
                        out=x1[:, GC * k:GC * (k + 1)].rearrange("p g w -> p (g w)"), in0=banks, scalar=q[:, 0:1],
                        in1=xb[k % RING][:].rearrange("p g w -> p (g w)"), op0=ALU.mult, op1=ALU.add).then_inc(x1_out, 1)
                    dve.wait_ge(x1_out, NC * b + k + 1)
                    for h in range(2):
                        last = nc.vector.bn_stats(bs[:, 2 * k + h, :],
                                                  x1[:, GC * k + 2 * h:GC * k + 2 * h + 2].rearrange("p g w -> p (g w)"))
                    last.then_inc(bn_out, 1)
                else:
                    wait(dve, o_st[k % 2], 16 * J * ((NC // 2) * b + k // 2))
                    nc.vector.scalar_tensor_tensor(
                        out=ob[k % 2][:].rearrange("p g w -> p (g w)"), in0=banks, scalar=q[:, 1:2],
                        in1=x1[:, GC * k:GC * (k + 1)].rearrange("p g w -> p (g w)"), op0=ALU.mult, op1=ALU.add
                        ).then_inc(o_out, 1)

            def statistics(b):
                m = LINKS * b
                dve.wait_ge(bn_out, NC * b + NC)
                nc.vector.tensor_copy(pad[:], bs[:, 0, 0:1])
                nc.vector.bn_aggr(mv[:], bs[:].rearrange("p n s -> p (n s)")).then_inc(own, 1)
                dve.wait_ge(own, m + 1)
                nc.vector.tensor_tensor(mc[:], mv[:, 0:1], b3p[:], ALU.subtract).then_inc(mean_in, 1)
                dve.wait_ge(mean_in, 2 * b + 1)
                dve.wait_ge(mean_out, 2 * b + 1)
                nc.vector.tensor_tensor(dm[:], mc[:], ps_s[:, 0:1], ALU.subtract).then_inc(own, 1)
                dve.wait_ge(own, m + 2)
                nc.vector.scalar_tensor_tensor(out=vv[:], in0=dm[:], scalar=dm[:, 0:1], in1=mv[:, 1:2],
                                               op0=ALU.mult, op1=ALU.add).then_inc(mean_in, 1)
                dve.wait_ge(std_out, b + 1)
                nc.vector.reciprocal(sc1[:, 0:1], sd[:]).then_inc(own, 1)
                nc.vector.tensor_tensor(ns[:], b3p[:], ps_s[:, 0:1], ALU.add).then_inc(own, 1)
                dve.wait_ge(own, m + 4)
                nc.vector.tensor_scalar(dm[:], ns[:], -1.0, None, ALU.mult).then_inc(own, 1)
                dve.wait_ge(own, m + 5)
                nc.vector.tensor_tensor(sc1[:, 1:2], dm[:], sc1[:, 0:1], ALU.mult).then_inc(norm_out, 1)

            def body(b, last=False):
                for k in range(NC):
                    evacuate(0, b, k)
                    if k == 0 and not last:
                        constant_mode(b + 1)
                statistics(b)
                if not last:
                    for i in range(IP):
                        invert(b + 1, i, (IP + NC + i) % NP)
                for k in range(NC):
                    evacuate(1, b, k)

            constant_mode(0)
            for i in range(IP):
                invert(0, i, i % NP)
            peeled(dve, body)

        @block.tensor
        def _(pe):
            def moving(a, buf, hl, g, dx):
                g %= GR
                c = slice(X0 + dx, X0 + dx + W)
                if g + 2 <= GR:
                    return [(0, 2, buf[a][:, hl, g:g + 2, c])]
                return [(0, 1, buf[a][:, hl, g:g + 1, c]), (1, 1, buf[a][:, hl, 0:1, c])]

            def chunk_ready(a, b, k):
                if k < NC:
                    pe.wait_ge(mid_in[a][k % RING], mid_count(a, b, k // RING, k % RING))
                else:
                    pe.wait_ge(below[a], (32 if a == 0 else 16) * (b + 1))
                if a == 1 and k == 0:
                    pe.wait_ge(above, 16 * (b + 1))

            def layer0(b, p):
                k = p // 2
                bank = bank_of(IP + k) + p % 2
                if p % 2 == 0:
                    chunk_ready(0, b, k)
                    if k >= NP:
                        pe.wait_ge(x1_out, NC * b + k - NP + 1)
                    elif isinstance(b, int) and b == 0:
                        pe.wait_ge(inv_lo, IP - NP + k + 1)
                    else:
                        pe.wait_ge(o_out, NC * b + k - NP + 1)
                else:
                    chunk_ready(0, b, k + 1)
                if p == 0:
                    pe.wait_ge(inv_lo, IP * (b + 1))
                g = 2 * p
                for dx in range(2):
                    for wl, xl in ((0, 0), (1, 0), (0, 1)):
                        for half, buf, gg in ((0, win, g), (1, mid, g + 1)):
                            for at, count, rhs in moving(0, buf, xl, gg, dx):
                                nc.tensor.matmul(ps[64 * half:64 * half + 64, bank, W * at:W * (at + count)],
                                                 lw0[:, wl, dx].rearrange("p m o -> p (m o)"), rhs,
                                                 start=(dx == wl == xl == at == 0), stop=False, skip_group_check=True)
                for i in range(2):
                    for hl in range(2):
                        r = J * (g + i)
                        last = nc.tensor.matmul(ps[:, bank, W * i:W * (i + 1)],
                                                gi[:, r:r + J, :].rearrange("p h o -> p (h o)"), iw[:, hl, :],
                                                start=False, stop=(i == hl == 1), skip_group_check=True)
                last.then_inc(conv[0], 1)

            def layer1(b, p, last_image):
                k = p // 2
                bank = bank_of(2 * IP + NC + k) + p % 2
                if p % 2 == 0:
                    chunk_ready(1, b, k)
                    if k >= NP:
                        pe.wait_ge(o_out, NC * b + k - NP + 1)
                    elif last_image:
                        pe.wait_ge(x1_out, NC * b + NC)
                    else:
                        pe.wait_ge(inv_lo, IP * (b + 1) + IP - NP + k + 1)
                else:
                    chunk_ready(1, b, k + 1)
                g = 2 * p
                for dx in range(3):
                    for wl, xl in ((0, 0), (1, 0), (0, 1)):
                        for j, variant, buf, gg in ((0, 0, mid, g), (1, 1, win, g), (2, 0, win, g), (3, 1, mid, g + 1)):
                            for at, count, rhs in moving(1, buf, xl, gg, dx - 1):
                                last = nc.tensor.matmul(ps[32 * j:32 * j + 32, bank, W * at:W * (at + count)],
                                                        lw1[:, wl, variant, dx, :], rhs,
                                                        start=(dx == wl == xl == at == 0),
                                                        stop=(dx == 2 and xl == 1), skip_group_check=True)
                last.then_inc(conv[1], 1)

            def bank_of(i):
                return 2 * (i % NP)

            def invert(b, i, bank):
                if i == 0:
                    pe.wait_ge(gm_dc, b + 1)
                if i >= NP:
                    pe.wait_ge(inv_lo, IP * b + i - NP + 1)
                elif not (isinstance(b, int) and b == 0):
                    pe.wait_ge(x1_out, NC * b - NP + i + 1)
                for bk in range(2):
                    for c in range(2):
                        for t in range(4):
                            o = 8 * i + 4 * bk + 2 * c + t // 2
                            last = nc.tensor.matmul(
                                ps[32 * t:32 * t + 32, bank + bk, H * c:H * (c + 1)],
                                gm[:, :, o], ih[:, t % 2, :], start=(c == 0), stop=(c == 1), skip_group_check=True)
                last.then_inc(inv_ps, 1)

            def body(b, last=False):
                for p in range(2 * NC):
                    layer0(b, p)
                for i in range(2):
                    pe.wait_ge(mean_in, 2 * b + i + 1)
                    nc.tensor.matmul(ps_s[:, i:i + 1], mats[:, 0, :], (mc, vv)[i][:], start=True, stop=True
                                     ).then_inc(mean_out, 1)
                if not last:
                    for i in range(IP):
                        n = IP + NC + i
                        invert(b + 1, i, bank_of(n))
                for p in range(2 * NC):
                    layer1(b, p, last)

            for i in range(IP):
                invert(0, i, bank_of(i))
            peeled(pe, body)


def setup(nc, cw, cb, w3, b3, t_inv_h, t_inv_w, mats, gmax, stat_d, win, mid, ih, iw, lw0, lw1,
          sc0, eps, b3p, dc, q, ps_s):
    with ExitStack() as ctx:
        def sb(name, shape, dt):
            return ctx.enter_context(nc.sbuf_tensor(f"su_{name}", shape, dt))

        def sem(name):
            return ctx.enter_context(nc.semaphore(f"su_{name}"))

        c0 = sb("c0", [P, 3, C], F32)
        c1 = sb("c1", [P, C, 9], F32)
        t0 = sb("t0", [P, 3, C], F32)
        z = sb("z", [P, 3 * C], F32)
        h0 = sb("h0", [P, 2, 3, C], F16)
        h1 = sb("h1", [P, 2, 9, C], F16)
        mx = sb("mx", [P, 4], F32)
        row = sb("row", [1, 4], F32)
        cbr = sb("cbr", [1, 2, C], F32)
        ones = sb("ones", [1, P], F32)
        LOADS = 16 * (6 * J + 4)
        loaded = sem("loaded")
        own = sem("own_setup")
        max_ps = sem("max_ps")
        max_row = sem("max_row")
        cleared = sem("cleared")
        block = ctx.enter_context(nc.Block())

        @block.sync
        def _(sp):
            n = 0
            with nc.allow_non_contiguous_dma("weights are gathered once"):
                for j in range(J):
                    s = slice(32 * j, 32 * j + 32)
                    for t in range(3):
                        sp.dma_start(c0[s, t, :], cw[:, C * t:C * (t + 1)].rearrange("o c -> c o")).then_inc(loaded, 16)
                    sp.dma_start(c1[s], w3.rearrange("o c y x -> c o (y x)")).then_inc(loaded, 16)
                    sp.dma_start(sc0[s], stat_d.rearrange("b t c -> c b t")).then_inc(loaded, 16)
                    sp.dma_start(b3p[s], b3.rearrange("(c u) -> c u", u=1)).then_inc(loaded, 16)
                    n += 6
            sp.dma_start(ih[:], t_inv_h).then_inc(loaded, 16)
            sp.dma_start(iw[:], t_inv_w).then_inc(loaded, 16)
            sp.dma_start(cbr[:, 0, :], cb.rearrange("(u c) -> u c", u=1)).then_inc(loaded, 16)
            sp.dma_start(cbr[:, 1, :], b3.rearrange("(u c) -> u c", u=1)).then_inc(loaded, 16)
            assert 16 * (n + 4) == LOADS
            sp.wait_ge(loaded, LOADS)

        @block.gpsimd
        def _(pool):
            for t in (*win, *mid):
                last = nc.gpsimd.memset(t[:].rearrange("p a g w -> p (a g w)"), 0.0)
                last.then_inc(cleared, 1)

        @block.tensor
        def _(pe):
            pe.wait_ge(max_row, 1)
            for i in range(2):
                nc.tensor.matmul(ps_s[0:1, P * i:P * (i + 1)], mx[:, i:i + 1], mats[:, 2, :], start=True, stop=True
                                 ).then_inc(max_ps, 1)
            pe.wait_ge(max_row, 2)
            nc.tensor.matmul(ps_s[:, 256:258], ones[0:1, :], row[0:1, 0:2], start=True, stop=True).then_inc(max_ps, 1)

        @block.vector
        def _(dve):
            count = [0]

            def link(ins):
                count[0] += 1
                ins.then_inc(own, 1)
                dve.wait_ge(own, count[0])

            V = nc.vector
            V.memset(eps[:], EPS)
            V.memset(ones[:], 1.0)
            V.memset(lw0[:].rearrange("p a b c d -> p (a b c d)"), 0.0)
            V.memset(lw1[:].rearrange("p a b c d -> p (a b c d)"), 0.0)
            dve.wait_ge(loaded, LOADS)
            link(V.tensor_tensor(dc[:], cbr[:, 0, :], cbr[:, 1, :], ALU.add))
            link(V.tensor_scalar(dc[:], dc[:], float(H * W), None, ALU.mult))
            link(V.tensor_tensor(z[:, 0:C], c0[:, 0, :], c0[:, 1, :], ALU.subtract))
            link(V.tensor_tensor(t0[:, 0, :], z[:, 0:C], c0[:, 2, :], ALU.subtract))
            link(V.tensor_copy(t0[:, 1:3, :], c0[:, 1:3, :]))
            link(V.memset(mx[:], 0.0))
            link(V.tensor_reduce(mx[0:1, 2:3], dc[:], AX_X, ALU.max, apply_absolute_value=True))
            link(V.tensor_tensor(mx[:, 2:3], mx[:, 2:3], gmax[:], ALU.add))
            link(V.tensor_scalar(mx[:, 2:3], mx[:, 2:3], 128.0 / (H * W), 1e-30, ALU.mult, ALU.max))
            link(V.tensor_reduce(mx[:, 0:1], t0[:].rearrange("p t o -> p (t o)"), AX_X, ALU.max, apply_absolute_value=True))
            link(V.tensor_tensor(mx[:, 0:1], mx[:, 0:1], mx[:, 2:3], ALU.max))
            link(V.tensor_reduce(mx[:, 1:2], c1[:].rearrange("p o t -> p (o t)"), AX_X, ALU.max, apply_absolute_value=True))
            V.tensor_scalar(mx[:, 1:2], mx[:, 1:2], 1e-30, None, ALU.max).then_inc(max_row, 1)
            dve.wait_ge(max_ps, 2)
            link(V.tensor_reduce(row[:, 2:4], ps_s[0:1, 0:2 * P].rearrange("p (a b) -> p a b", a=2), AX_X, ALU.max))
            V.tensor_scalar(row[:, 0:2], row[:, 2:4], 1.0 / 64, None, ALU.mult).then_inc(max_row, 1)
            dve.wait_ge(max_ps, 3)
            link(V.tensor_copy(q[:, 0:2], ps_s[:, 256:258]))
            link(V.reciprocal(q[:, 2:4], q[:, 0:2]))
            link(V.tensor_scalar(ih[:], ih[:], q[:, 2:3], None, ALU.mult))
            link(V.tensor_scalar(t0[:], t0[:], q[:, 2:3], None, ALU.mult))
            link(V.tensor_scalar(c1[:], c1[:], q[:, 3:4], None, ALU.mult))
            link(V.tensor_copy(h0[:, 0], t0[:]))
            link(V.tensor_tensor(h0[:, 1], t0[:], h0[:, 0], ALU.subtract))
            link(V.tensor_copy(h1[:, 0], c1[:].rearrange("p o t -> p t o")))
            link(V.tensor_tensor(h1[:, 1], c1[:].rearrange("p o t -> p t o"), h1[:, 0], ALU.subtract))
            for m in range(2):
                for blk, tap, dx in ((m, 0, 0), (m + 1, 1, 0), (m, 2, 1)):
                    s = slice(32 * blk, 32 * blk + 32)
                    link(V.tensor_copy(lw0[s, :, dx, m, :], h0[s, :, tap, :]))
            for variant in range(2):
                for dy in range(3):
                    s = slice(32 * (dy + 1 - variant), 32 * (dy + 2 - variant))
                    link(V.tensor_copy(lw1[s, :, variant, :, :], h1[s, :, 3 * dy:3 * dy + 3, :]))


_INS = ["x", "L0_conv_conv_w", "L0_conv_conv_b", "L0_conv_w1r", "L0_conv_w1i", "L0_conv_w2r", "L0_conv_w2i",
        "L1_conv_weight", "L1_conv_bias"]


def kernel(**inputs):
    import numpy as _np
    import concourse.bacc as _bacc
    from concourse import mybir as _mybir
    from concourse.bass_utils import run_bass_kernel_spmd as _run

    nc = _bacc.Bacc("TRN2", target_bir_lowering=False, num_devices=1)
    arrays, args = {}, []
    data = {name: inputs[name] for name in _INS}
    data.update(tables())
    for name, a in data.items():
        a = _np.ascontiguousarray(a)
        arrays[f"in_{name}_dram"] = a
        args.append(nc.dram_tensor(f"in_{name}_dram", a.shape, _mybir.dt.from_np(a.dtype), kind="ExternalInput").ap())
    args.append(nc.dram_tensor("out_0_dram", (B, C, H, W), _mybir.dt.float32, kind="ExternalOutput").ap())
    program(nc, *args)
    r = _run(nc, [arrays], core_ids=[0])
    return r.results[0]["out_0_dram"]
```

```python
from contextlib import ExitStack

import numpy as np

import concourse.bass as bass
from concourse import mybir

F32 = mybir.dt.float32
F16 = mybir.dt.float16
ALU = mybir.AluOpType
ACT = mybir.ActivationFunctionType
AX_X = mybir.AxisListType.X

B, C, H, W = 16, 32, 256, 256
M1, M2 = 32, 32
P = 128
EPS = 1e-5

CC = 4
NQ = C // CC
NG = CC // 2
NK = M1 + 1
KS = 4
KP = -(-NK // KS) * KS
KQ = KP // KS
YK = NK + KP
AHEAD = 4
NHI = 4
CA = 3
ND = 4 * KS

TQ = 4
NT = M1 // TQ
MJ = 4
MM = M2 // MJ

J = 4
GC = 4
NC = H // (J * GC)
RING = 4
GR = RING * GC
WP = W + 4
X0 = 2
NP = 3
NQD = NC // RING
IP = 4


SH = 128.0
SF = 4096.0
SY = 8.0
SW = 16384.0


def tables():
    def split(a):
        hi = a.astype(np.float16)
        return hi, (a - hi.astype(np.float64)).astype(np.float16)

    n = np.arange(256)
    ang = 2 * np.pi / 256
    fwd_h = np.concatenate([np.cos(ang * np.outer(n, np.arange(NK))), np.sin(ang * np.outer(n, np.arange(NK)))], 1)
    fwd_h = fwd_h.reshape(2, P, 2 * NK).transpose(1, 0, 2)
    th = np.stack(split(SF * fwd_h), 1)
    phi = ang * np.outer(n, np.arange(M2))
    c, s = np.cos(phi), np.sin(phi)
    of_cos = np.stack([np.stack([c, -s], 1)] * 2, 1)
    of_sin = np.stack([np.stack([-s, -c], 1), np.stack([s, c], 1)], 1)
    fwd_w = np.stack([of_cos, of_sin]).reshape(2, 2, P, 4 * M2).transpose(2, 0, 1, 3)
    tw = np.stack(split(SF * fwd_w), 1)
    kx = np.concatenate([np.arange(M1), -1 - np.arange(M1)])
    the = ang * np.outer(kx, n)
    inv_h = np.stack([np.concatenate([np.cos(the), -np.sin(the)]),
                      np.concatenate([np.sin(the), np.cos(the)])], 1) / (H * W)
    amp = np.where(np.arange(M2) == 0, 1.0, 2.0)[:, None]
    inv_w = np.concatenate([amp * np.cos(phi.T), -amp * np.sin(phi.T)])
    iw = np.concatenate([inv_w, inv_w])
    ch = np.arange(P) % C
    mean_of_group = (ch[:, None] // 2 == ch[None, :] // 2) / (2.0 * J)
    mats = np.stack([mean_of_group, np.full((P, P), 1.0 / P), np.eye(P)], 1)
    return {"t_fwd_h": np.ascontiguousarray(th), "t_fwd_w": np.ascontiguousarray(tw),
            "t_inv_h": inv_h.astype(np.float32), "t_inv_w": iw.astype(np.float32),
            "t_mats": mats.astype(np.float32)}


def wait(eng, sem, count):
    if not (isinstance(count, int) and count <= 0):
        eng.wait_ge(sem, count)


def program(nc, x, cw, cb, w1r, w1i, w2r, w2i, w3, b3, t_fwd_h, t_fwd_w, t_inv_h, t_inv_w, t_mats, out):
    stat_d = nc.dram_tensor("stat_scratch", [B, 2, C], F32).ap()
    modes_d = nc.dram_tensor("modes_scratch", [MJ, 2, B, 2, M1, MM * C], F32).ap()
    with ExitStack() as ctx:
        gmax = ctx.enter_context(nc.sbuf_tensor("gmax", [P, 1], F32))
        mats = ctx.enter_context(nc.sbuf_tensor("mats", [P, 3, P], F32))
        with ExitStack() as both:
            modes = both.enter_context(nc.sbuf_tensor("modes", [P, B, KS, M1 // KS, M2], F32))
            spectra(nc, x, t_fwd_h, t_fwd_w, t_mats, mats, modes, stat_d)
            mixing(nc, w1r, w1i, w2r, w2i, modes, modes_d, gmax)
        images(nc, x, cw, cb, w3, b3, t_inv_h, t_inv_w, mats, gmax, stat_d, modes_d, out)


def spectra(nc, x, t_fwd_h, t_fwd_w, t_mats, mats, modes, stat_d):
    N = B * NQ
    with ExitStack() as ctx:
        def sb(name, shape, dt):
            return ctx.enter_context(nc.sbuf_tensor(f"sp_{name}", shape, dt))

        def sem(name):
            return ctx.enter_context(nc.semaphore(f"sp_{name}"))

        xt = [sb(f"xt{i}", [P, CC, 2, W], F32) for i in range(NQ)]
        hi = [sb(f"hi{i}", [P, CC, 2, W], F16) for i in range(NHI)]
        lo = [sb(f"lo{i}", [P, CC, 2, W], F16) for i in range(2)]
        th = sb("th", [P, 2, 2, 2 * NK], F16)
        tw = sb("tw", [P, 2, 2, 2, 4 * M2], F16)
        y = [sb(f"y{i}", [P, 2, 2, YK, C], F16) for i in range(2)]
        xi = sb("xi", [P, 2, 2, KQ, M2], F32)
        st = sb("st", [P, CC, 6], F32)
        mv = sb("mv", [P, NG, 2], F32)
        pad = sb("pad", [P, 1], F32)
        dm = sb("dm", [P, NG], F32)
        nm = sb("nm", [P, 2, NG], F32)
        sq = sb("sq", [P, NG], F32)
        vv = sb("vv", [P, NG], F32)
        sd = sb("sd", [P, NG], F32)
        hv = sb("hv", [P, NG], F32)
        rs = sb("rs", [P, NG], F32)
        eps = sb("eps", [P, 1], F32)
        sn = sb("sn", [P, 2, NQ, NG], F32)
        sa = sb("sa", [1, B, 2, C], F32)
        ps_y = [ctx.enter_context(nc.psum_tensor(f"ps_y{i}", [P, 512], F32)) for i in range(4)]
        ps_x = ctx.enter_context(nc.psum_tensor("ps_x", [P, 3, 512], F32))
        ps_s = ctx.enter_context(nc.psum_tensor("ps_s", [P, 2, 256], F32))

        tables_in = sem("tables_in")
        x_in = [sem(f"x_in{i}") for i in range(NQ)]
        ready = sem("ready")
        bn_out = sem("bn_out")
        own = sem("own_chain")
        stats_in = sem("stats_in")
        stats_out = sem("stats_out")
        std_out = sem("std_out")
        norm_out = sem("norm_out")
        h_out = sem("h_out")
        hi_d = sem("hi_d")
        hi_a = sem("hi_a")
        lo_out = sem("lo_out")
        y_ps = sem("y_ps")
        y_hi = sem("y_hi")
        y_lo = sem("y_lo")
        x_ps = sem("x_ps")
        x_sb = sem("x_sb")
        moved = sem("moved")
        kept = sem("kept")
        stat_st = sem("stat_st")
        block = ctx.enter_context(nc.Block())

        @block.sync
        def _(sp):
            sp.dma_start(th[:], t_fwd_h).then_inc(tables_in, 16)
            sp.dma_start(tw[:], t_fwd_w).then_inc(tables_in, 16)
            sp.dma_start(mats[:], t_mats).then_inc(tables_in, 16)

            def load(b, q):
                sp.dma_start(xt[q][:].rearrange("p c a w -> p (c a) w"),
                             x[b, CC * q:CC * (q + 1)].rearrange("c (a p) w -> p (c a) w", a=2)).then_inc(x_in[q], 16)

            def store_statistics():
                sp.wait_ge(kept, 2 * B)
                sp.dma_start(stat_d.rearrange("(u b) t c -> u (b t c)", u=1), sa[:].rearrange("p b t c -> p (b t c)")
                             ).then_inc(stat_st, 16)

            def place(b, kk):
                if kk == 0:
                    sp.wait_ge(x_sb, b + 1)
                for s, q0, k0 in ((0, 0, kk), (1, int(kk == 0), (kk - 1) % KS)):
                    for ri in range(2):
                        sp.dma_start(modes[64 * s + 32 * ri:64 * s + 32 * ri + 32, b, k0],
                                     xi[32 * kk:32 * kk + 32, s, ri, q0:q0 + M1 // KS, :]).then_inc(moved, 16)

            for q in range(NQ):
                load(0, q)
            for q in range(NQ):
                sp.wait_ge(lo_out, q + 1)
                load(1, q)
            for q in range(NQ):
                sp.wait_ge(lo_out, NQ + q + 1)
                load(2, q)
            with sp.Fori(2, B - 1) as b:
                for q in range(NQ):
                    sp.wait_ge(lo_out, NQ * b + q + 1)
                    load(b + 1, q)
                    if q < KS:
                        place(b - 2, q)
            for b in (B - 3, B - 2, B - 1):
                for kk in range(KS):
                    place(b, kk)
            store_statistics()
            sp.wait_ge(moved, 16 * ND * B)
            sp.wait_ge(stat_st, 16)

        def images_in_pairs(eng, step):
            def pair(h):
                for par in range(2):
                    for q in range(NQ):
                        step(2 * h + par, q, par)

            pair(0)
            with eng.Fori(1, B // 2 - 1) as h:
                pair(h)
            pair(B // 2 - 1)

        def later(b, q, k):
            return b + (q + k) // NQ, (q + k) % NQ

        def exists(b, q, k):
            return not isinstance(b, int) or 0 <= NQ * b + q + k < N

        @block.gpsimd
        def _(pool):
            def step(b, q, par):
                n = NQ * b + q
                pool.wait_ge(hi_d, n + 1)
                pool.wait_ge(hi_a, n + 1)
                wait(pool, y_ps, 2 * (n - 1))
                nc.gpsimd.tensor_tensor(lo[q % 2][:], xt[q][:], hi[q % NHI][:], ALU.subtract).then_inc(lo_out, 1)

            images_in_pairs(pool, step)

        @block.scalar
        def _(act):
            act.wait_ge(ready, 3)

            def root(b, q):
                n = NQ * b + q
                act.wait_ge(stats_out, 2 * n + 2)
                nc.scalar.activation(sd[:], ps_s[:, 1, 0:NG], ACT.Sqrt, bias=eps[:, 0:1],
                                     scale=SH ** -2).then_inc(std_out, 1)

            def normalise(b, q):
                act.wait_ge(norm_out, NQ * b + q + 1)
                for g in range(NG):
                    v = xt[q][:, 2 * g:2 * g + 2, :, :].rearrange("p c a w -> p (c a w)")
                    last = nc.scalar.activation(v, v, ACT.Identity, bias=sn[:, 1, q, g:g + 1], scale=sn[:, 0, q, g:g + 1])
                last.then_inc(h_out, 1)

            def high(b, q):
                n = NQ * b + q
                act.wait_ge(h_out, n + 1)
                wait(act, y_ps, 2 * (n - NHI + 1))
                nc.scalar.copy(hi[q % NHI][:, 0:CA], xt[q][:, 0:CA]).then_inc(hi_a, 1)

            def y_high(b, q, par):
                if q == 0:
                    wait(act, x_ps, b - 1)
                for wh in range(2):
                    act.wait_ge(y_ps, 2 * (NQ * b + q) + wh + 1)
                    nc.scalar.mul(y[par][:, 0, wh, 0:2 * NK, CC * q:CC * (q + 1)].rearrange("p k c -> p c k"),
                                  ps_y[2 * (q % 2) + wh][:, 0:CC * 2 * NK].rearrange("p (c k) -> p c k", c=CC),
                                  SY / (SH * SF)).then_inc(y_hi, 1)

            def modes_out(b):
                act.wait_ge(x_ps, b + 1)
                wait(act, moved, 16 * ND * b)
                for i in range(3):
                    w = min(4, KQ - 4 * i)
                    for part in range(4):
                        last = nc.scalar.mul(xi[:, part // 2, part % 2, 4 * i:4 * i + w],
                                             ps_x[:, i, 0:w * P].rearrange("p (q r k) -> p r q k", q=w, r=4)[:, part],
                                             1.0 / (SY * SF))
                last.then_inc(x_sb, 1)

            def step(b, q, par):
                if exists(b, q, AHEAD):
                    root(*later(b, q, AHEAD))
                if exists(b, q, -1):
                    y_high(*later(b, q, -1), par if q else 1 - par)
                if exists(b, q, AHEAD - 2):
                    normalise(*later(b, q, AHEAD - 2))
                    high(*later(b, q, AHEAD - 2))
                if q == NQ - 1 and exists(b, q, -NQ):
                    modes_out(b - 1)

            for n in range(AHEAD):
                root(0, n)
                if n >= 2:
                    normalise(0, n - 2)
                    high(0, n - 2)
            images_in_pairs(act, step)
            y_high(B - 1, NQ - 1, 1)
            modes_out(B - 1)

        LINKS = 7

        @block.vector
        def _(dve):
            nc.vector.memset(eps[:], EPS / SH ** 2).then_inc(ready, 1)
            for t in y:
                nc.vector.memset(t[:, :, :, 2 * NK:YK, :].rearrange("p a b k d -> p (a b) (k d)"), 0.0).then_inc(ready, 1)
            dve.wait_ge(ready, 3)

            def rows_of(b, q, c):
                if c == 0:
                    dve.wait_ge(x_in[q], 16 * b + 16)
                ins = nc.vector.bn_stats(st[:, c, :], xt[q][:, c].rearrange("p a w -> p (a w)"))
                if c == CC - 1:
                    ins.then_inc(bn_out, 1)

            def rows_of_groups(b, q):
                dve.wait_ge(bn_out, NQ * b + q + 1)
                nc.vector.tensor_copy(pad[:], st[:, 0, 0:1])
                for g in range(NG):
                    last = nc.vector.bn_aggr(mv[:, g, :], st[:, 2 * g:2 * g + 2, :].rearrange("p a b -> p (a b)"))
                last.then_inc(stats_in, 1)

            def scale(b, q, between=()):
                n = NQ * b + q
                m = LINKS * n
                between = iter(between)
                mean, var = (ps_s[:, i, 0:NG] for i in range(2))

                def work():
                    for piece in next(between, ()):
                        piece()

                work()
                dve.wait_ge(stats_in, 2 * n + 1)
                dve.wait_ge(stats_out, 2 * n + 1)
                nc.vector.tensor_tensor(dm[:], mv[:, :, 0], mean, ALU.subtract).then_inc(own, 1)
                nc.vector.tensor_scalar(nm[:, q % 2], mean, -1.0, None, ALU.mult)
                work()
                dve.wait_ge(own, m + 1)
                nc.vector.tensor_tensor(sq[:], dm[:], dm[:], ALU.mult).then_inc(own, 1)
                work()
                dve.wait_ge(own, m + 2)
                nc.vector.tensor_tensor(vv[:], sq[:], mv[:, :, 1], ALU.add).then_inc(stats_in, 1)
                work()
                dve.wait_ge(std_out, n + 1)
                nc.vector.tensor_scalar(hv[:], var, 0.5 / SH ** 2, 0.5 * EPS / SH ** 2, ALU.mult, ALU.add).then_inc(own, 1)
                nc.vector.reciprocal(rs[:], sd[:]).then_inc(own, 1)
                work()
                dve.wait_ge(own, m + 4)
                nc.vector.tensor_tensor(hv[:], hv[:], rs[:], ALU.mult).then_inc(own, 1)
                work()
                dve.wait_ge(own, m + 5)
                nc.vector.scalar_tensor_tensor(out=rs[:], in0=sd[:], scalar=0.5, in1=hv[:], op0=ALU.mult, op1=ALU.add
                                               ).then_inc(own, 1)
                work()
                dve.wait_ge(own, m + 6)
                nc.vector.reciprocal(sn[:, 0, q, :], rs[:]).then_inc(own, 1)
                dve.wait_ge(own, m + 7)
                nc.vector.tensor_tensor(sn[:, 1, q, :], nm[:, q % 2], sn[:, 0, q, :], ALU.mult).then_inc(norm_out, 1)
                if q == NQ - 1:
                    dve.wait_ge(norm_out, n + 1)
                    for r in range(2):
                        nc.vector.tensor_copy(sa[:, bass.ds(b, 1), :, r:C:2].rearrange("p u t n -> p (u t) n"),
                                              sn[0:1].rearrange("p t q g -> p t (q g)")).then_inc(kept, 1)

            def high(b, q):
                n = NQ * b + q
                dve.wait_ge(h_out, n + 1)
                wait(dve, y_ps, 2 * (n - NHI + 1))
                nc.vector.tensor_copy(hi[q % NHI][:, CA:CC], xt[q][:, CA:CC]).then_inc(hi_d, 1)

            def y_low(b, q, par, wh):
                dve.wait_ge(y_hi, 2 * (NQ * b + q) + wh + 1)
                c = slice(CC * q, CC * (q + 1))
                nc.vector.scalar_tensor_tensor(
                    out=y[par][:, 1, wh, 0:2 * NK, c].rearrange("p k c -> p c k"),
                    in0=ps_y[2 * (q % 2) + wh][:, 0:CC * 2 * NK].rearrange("p (c k) -> p c k", c=CC),
                    scalar=SY / (SH * SF), in1=y[par][:, 0, wh, 0:2 * NK, c].rearrange("p k c -> p c k"),
                    op0=ALU.mult, op1=ALU.subtract).then_inc(y_lo, 1)

            def step(b, q, par):
                his = [lambda: high(*later(b, q, AHEAD - 3))] if exists(b, q, AHEAD - 3) else []
                low = [[lambda wh=wh: y_low(*later(b, q, -2), par if q > 1 else 1 - par, wh)]
                       if exists(b, q, -2) else [] for wh in range(2)]
                bn = [[lambda c=c: rows_of(*later(b, q, AHEAD + 1), c)]
                      if exists(b, q, AHEAD + 1) else [] for c in range(CC)]
                aggr = [lambda: rows_of_groups(*later(b, q, AHEAD + 1))] if exists(b, q, AHEAD + 1) else []
                pieces = [low[0], low[1], his, bn[0] + bn[1], bn[2], bn[3], aggr]
                if exists(b, q, AHEAD):
                    scale(*later(b, q, AHEAD), pieces)
                else:
                    for piece in sum(pieces, []):
                        piece()

            def rows_first(q):
                for c in range(CC):
                    rows_of(0, q, c)
                rows_of_groups(0, q)

            for q in range(AHEAD):
                rows_first(q)
                scale(0, q)
            rows_first(AHEAD)
            for q in range(AHEAD - 3):
                high(0, q)
            images_in_pairs(dve, step)
            for q in (NQ - 2, NQ - 1):
                for wh in range(2):
                    y_low(B - 1, q, 1, wh)

        @block.tensor
        def _(pe):
            pe.wait_ge(tables_in, 48)
            pe.wait_ge(ready, 3)

            def mean(b, q, i):
                pe.wait_ge(stats_in, 2 * (NQ * b + q) + i + 1)
                nc.tensor.matmul(ps_s[:, i, 0:NG], mats[:, 1, :], (mv[:, :, 0], vv[:])[i],
                                 start=True, stop=True).then_inc(stats_out, 1)

            def along_h(b, q, wh):
                n = NQ * b + q
                if wh == 0:
                    pe.wait_ge(lo_out, n + 1)
                wait(pe, y_lo, 2 * (n - 2) + wh + 1)
                for c in range(CC):
                    o = ps_y[2 * (q % 2) + wh][:, 2 * NK * c:2 * NK * (c + 1)]
                    k = 0
                    for hh in range(2):
                        for part, hl in ((hi[q % NHI], 0), (hi[q % NHI], 1), (lo[q % 2], 0)):
                            last = nc.tensor.matmul(o, part[:, c, hh, wh * P:(wh + 1) * P], th[:, hl, hh, :],
                                                    start=(k == 0), stop=(k == 5))
                            k += 1
                last.then_inc(y_ps, 1)

            def along_w(b, par, kq):
                if kq == 0:
                    pe.wait_ge(y_lo, 2 * NQ * b + 2 * NQ)
                    wait(pe, x_sb, b)
                k = 0
                for cs in range(2):
                    for wh in range(2):
                        for yl, tl in ((0, 0), (0, 1), (1, 0)):
                            last = nc.tensor.matmul(
                                ps_x[:, kq // 4, (kq % 4) * P:(kq % 4 + 1) * P],
                                y[par][:, yl, wh, NK * cs + KS * kq:NK * cs + KS * (kq + 1), :].rearrange("p k c -> p (k c)"),
                                tw[:, tl, cs, wh, :], start=(k == 0), stop=(k == 11))
                            k += 1
                if kq == KQ - 1:
                    last.then_inc(x_ps, 1)

            def step(b, q, par):
                if exists(b, q, AHEAD):
                    mean(*later(b, q, AHEAD), 1)
                along_h(b, q, 0)
                if 2 <= q and exists(b, q, -NQ):
                    along_w(b - 1, 1 - par, q - 2)
                if exists(b, q, AHEAD + 1):
                    mean(*later(b, q, AHEAD + 1), 0)
                along_h(b, q, 1)
                if q >= NQ - 3 and exists(b, q, -NQ):
                    along_w(b - 1, 1 - par, q + 1)

            mean(0, 0, 0)
            for q in range(AHEAD):
                mean(0, q, 1)
                mean(0, q + 1, 0)
            images_in_pairs(pe, step)
            for kq in range(KQ):
                along_w(B - 1, 1, kq)


def mixing(nc, w1r, w1i, w2r, w2i, modes, modes_d, gmax):
    with ExitStack() as ctx:
        def sb(name, shape, dt):
            return ctx.enter_context(nc.sbuf_tensor(f"mx_{name}", shape, dt))

        def sem(name):
            return ctx.enter_context(nc.semaphore(f"mx_{name}"))

        w = [sb(f"w{i}", [P, C, TQ, M2], F32) for i in range(2)]
        xx = [sb(f"xx{i}", [P, M2, 2, B], F32) for i in range(2)]
        g = [sb(f"g{i}", [P, 2, TQ, MM * C], F32) for i in range(2)]
        top = sb("top", [P, 1], F32)
        ps = [[ctx.enter_context(nc.psum_tensor(f"ps_m{i}{t}", [P, 512], F32)) for t in range(2)] for i in range(4)]

        w_in = [sem(f"w_in{i}") for i in range(2)]
        xx_a = sem("xx_a")
        xx_d = sem("xx_d")
        mixed = sem("mixed")
        g_out = sem("g_out")
        max_own = sem("max_own")
        g_st = [sem(f"g_st{i}") for i in range(2)]
        STORES = 16 * 2
        block = ctx.enter_context(nc.Block())

        def fill(copy, negate, dst, k, t, s):
            r, i = slice(64 * s, 64 * s + 32), slice(64 * s + 32, 64 * s + 64)

            def src(part):
                return modes[part, :, t, k, :].rearrange("p b k -> p k b")

            copy(dst[r, :, 0, :], src(r))
            copy(dst[r, :, 1, :], src(i))
            copy(dst[i, :, 1, :], src(r))
            return negate(dst[i, :, 0, :], src(i))

        @block.sync
        def _(sp):
            def load(k, slot):
                for part, src, t0 in ((0, w1r, TQ * k), (1, w1i, TQ * k),
                                      (2, w2r, M1 - TQ - TQ * k), (3, w2i, M1 - TQ - TQ * k)):
                    sp.dma_start(w[slot][32 * part:32 * part + 32], src[:, :, bass.ds(t0, TQ), :]).then_inc(w_in[slot], 16)

            def store(k, slot):
                sp.wait_ge(g_out, TQ * k + TQ)
                for s in range(2):
                    sp.dma_start(modes_d.rearrange("j r b s k n -> s (j r b) k n")[s, :, bass.ds(TQ * k, TQ), :],
                                 g[slot][:, s]).then_inc(g_st[slot], 16)

            load(0, 0)
            load(1, 1)
            with sp.Fori(0, NT // 2 - 1) as h:
                for slot in range(2):
                    sp.wait_ge(mixed, TQ * (2 * h + slot + 1))
                    load(2 * h + slot + 2, slot)
                    store(2 * h + slot, slot)
            for slot in range(2):
                store(NT - 2 + slot, slot)
            for slot in range(2):
                sp.wait_ge(g_st[slot], STORES * (NT // 2))

        def each_step(eng, body):
            for slot in range(2):
                body(0, slot)
            with eng.Fori(1, NT // 2) as h:
                for slot in range(2):
                    body(h, slot)

        @block.scalar
        def _(act):
            def evacuate(h, slot, t):
                k = 2 * h + slot
                act.wait_ge(mixed, TQ * k + t + 1)
                if t == 0:
                    wait(act, max_own, 2 * (k - 1))
                    wait(act, g_st[slot], STORES * h)
                for s in range(2):
                    last = nc.scalar.copy(g[slot][:, s, t, :], ps[t][s][:, 0:MM * C])
                last.then_inc(g_out, 1)

            def body(h, slot):
                for t in range(TQ):
                    n = TQ * (2 * h + slot) + t
                    wait(act, mixed, n - 1)
                    fill(nc.scalar.copy, lambda o, a: nc.scalar.mul(o, a, -1.0), xx[t % 2], 2 * h + slot, t, 1).then_inc(xx_a, 1)
                    if t:
                        evacuate(h, slot, t - 1)
                    elif slot:
                        evacuate(h, 0, TQ - 1)
                    elif not isinstance(h, int):
                        evacuate(h - 1, 1, TQ - 1)

            each_step(act, body)
            evacuate(NT // 2 - 1, 1, TQ - 1)

        @block.vector
        def _(dve):
            def largest(k, slot):
                dve.wait_ge(g_out, TQ * k + TQ)
                dve.wait_ge(max_own, 2 * k + 1)
                nc.vector.tensor_reduce(top[:], g[slot][:].rearrange("p s t k -> p (s t k)"), AX_X, ALU.max,
                                        apply_absolute_value=True).then_inc(max_own, 1)
                dve.wait_ge(max_own, 2 * k + 2)
                nc.vector.tensor_tensor(gmax[:], gmax[:], top[:], ALU.max).then_inc(max_own, 1)

            def body(h, slot):
                k = 2 * h + slot
                for t in range(TQ):
                    n = TQ * k + t
                    wait(dve, mixed, n - 1)
                    fill(nc.vector.tensor_copy,
                         lambda o, a: nc.vector.tensor_scalar(o, a, -1.0, None, ALU.mult), xx[t % 2], k, t, 0
                         ).then_inc(xx_d, 1)
                if not (isinstance(k, int) and k == 0):
                    largest(k - 1, 1 - slot)

            nc.vector.memset(gmax[:], 0.0).then_inc(max_own, 1)
            each_step(dve, body)
            largest(NT - 1, 1)
            dve.wait_ge(max_own, 2 * NT + 1)

        @block.tensor
        def _(pe):
            def body(h, slot):
                pe.wait_ge(w_in[slot], 64 * h + 64)
                for t in range(TQ):
                    n = TQ * (2 * h + slot) + t
                    pe.wait_ge(xx_d, n + 1)
                    pe.wait_ge(xx_a, n + 1)
                    wait(pe, g_out, n - TQ + 1)
                    nc.tensor.matmul(ps[t][0][0:32, 511:512], xx[t % 2][:, 0].rearrange("p r b -> p (r b)"),
                                     xx[t % 2][:, 0, 0, 0:1], start=True, stop=True)
                    for m in range(MM):
                        for s in range(2):
                            rows = slice(64 * s, 64 * s + 64)
                            for j in range(MJ):
                                ky = MM * j + m
                                last = nc.tensor.matmul(
                                    ps[t][s][32 * j:32 * j + 32, C * m:C * (m + 1)],
                                    xx[t % 2][rows, ky].rearrange("p r b -> p (r b)"),
                                    w[slot][rows, :, TQ - 1 - t if s else t, ky], start=True, stop=True)
                    last.then_inc(mixed, 1)

            each_step(pe, body)


def images(nc, x, cw, cb, w3, b3, t_inv_h, t_inv_w, mats, gmax, stat_d, modes_d, out):
    with ExitStack() as ctx:
        def sb(name, shape, dt):
            return ctx.enter_context(nc.sbuf_tensor(f"im_{name}", shape, dt))

        def sem(name):
            return ctx.enter_context(nc.semaphore(f"im_{name}"))

        win = [sb(f"win{a}", [P, 2, GR, WP], F16) for a in range(2)]
        mid = [sb(f"mid{a}", [P, 2, GR, WP], F16) for a in range(2)]
        x1 = sb("x1", [P, H // J, W], F32)
        hn = [sb(f"hn{i}", [P, GC, W + 1], F32) for i in range(2)]
        gi = sb("gi", [P, H, C], F16)
        gm = sb("gm", [P, M2, C], F32)
        ih = sb("ih", [P, 2, H], F32)
        iw = sb("iw", [P, 2, W], F16)
        lw0 = sb("lw0", [P, 2, 2, C], F16)
        lwr = sb("lwr", [P, 2, J, C], F16)
        lw1 = sb("lw1", [P, 2, 2, 3, C], F16)
        bs = sb("bs", [P, 2 * NC, 6], F32)
        sc0 = sb("sc0", [P, B, 2], F32)
        scc = sb("scc", [P, 2], F32)
        sc1 = sb("sc1", [P, 2], F32)
        mv = sb("mv", [P, 2], F32)
        mc = sb("mc", [P, 1], F32)
        pad = sb("pad", [P, 1], F32)
        dm = sb("dm", [P, 1], F32)
        vv = sb("vv", [P, 1], F32)
        sd = sb("sd", [P, 1], F32)
        hv = sb("hv", [P, 1], F32)
        rs = sb("rs", [P, 1], F32)
        ns = sb("ns", [P, 1], F32)
        eps = sb("eps", [P, 1], F32)
        b3p = sb("b3p", [P, 1], F32)
        dc = sb("dc", [1, C], F32)
        q = sb("q", [P, 4], F32)
        ps = ctx.enter_context(nc.psum_tensor("ps", [P, 2 * NP, 512], F32))
        ps_s = ctx.enter_context(nc.psum_tensor("ps_s3", [P, 512], F32))

        x_in = [sem(f"x1_in{i}") for i in range(2)]
        gm_in = sem("gm_in")

        def rows(t, b, kq, j):
            return t[b].rearrange("c (h k g j) w -> j c h k g w", j=J, g=2 * GC, k=2)[:, :, kq, j]

        def start_load(sp, b, kq, j):
            for r in range(J):
                sp.dma_start(x1[32 * r:32 * r + 32, bass.ds(4 * GC * kq + 2 * GC * j, 2 * GC), :],
                             rows(x, b, kq, j)[r]).then_inc(x_in[j], 16)

        def load_modes(sp, b):
            for r in range(2):
                sp.dma_start(gm[64 * r:64 * r + 64].rearrange("p (j m) o -> p j (m o)", j=MJ),
                             modes_d[:, r, b].rearrange("j s k n -> (s k) j n")).then_inc(gm_in, 16)

        def first_loads(sp):
            load_modes(sp, 0)
            for j in range(2):
                start_load(sp, 0, 0, j)

        setup(nc, cw, cb, w3, b3, t_inv_h, t_inv_w, mats, gmax, stat_d, win, mid, ih, iw, lw0, lwr, lw1,
              sc0, eps, b3p, dc, q, ps_s, first_loads)

        h_out = sem("hn_out")
        hi_out = sem("win_hi")
        lo_out = sem("win_lo")
        mid_in = [[sem(f"mid_in{a}{i}") for i in range(RING)] for a in range(2)]
        below = [sem("below0"), sem("below1")]
        above = sem("above1")
        conv = [sem("conv0"), sem("conv1")]
        inv_ps = sem("inv_ps")
        inv_hi = sem("inv_hi")
        inv_lo = sem("inv_lo")
        bn_out = sem("bn_out")
        x1_out = sem("x1_out")
        o_out = sem("o_out")
        o_st = [sem(f"o_st{i}") for i in range(2)]
        gm_dc = sem("gm_dc")
        own = sem("own3")
        mean_in = sem("mean_in")
        mean_out = sem("mean_out")
        scc_out = sem("scc_out")
        std_out = sem("std3_out")
        norm_out = sem("norm3_out")
        block = ctx.enter_context(nc.Block())

        def copies(a, slot):
            g0 = GC * slot
            r = [(mid[a][64:128, :, g0:g0 + GC, :], win[a][0:64, :, g0:g0 + GC, :])]
            if slot < RING - 1:
                r.append((mid[a][0:64, :, g0 + 1:g0 + GC + 1, :], win[a][64:128, :, g0:g0 + GC, :]))
            else:
                r.append((mid[a][0:64, :, g0 + 1:GR, :], win[a][64:128, :, g0:GR - 1, :]))
                r.append((mid[a][0:64, :, 0:1, :], win[a][64:128, :, GR - 1:GR, :]))
            return r

        def mid_count(a, b, kq, slot):
            return 16 * len(copies(a, slot)) * (NC // RING * b + kq + 1)

        zeros = sb("zeros", [P, 2, 1, WP], F16)
        zeroed = sem("zeroed")
        stepped = sem("stepped")

        def peeled(eng, body):
            body(0)
            with eng.Fori(1, B - 1) as b:
                body(b)
            body(B - 1, last=True)

        @block.sync
        def _(sp):
            def step_over():
                sp.sem_inc(stepped, 1)

            def load(b, kq, j):
                wait(sp, x_in[j], 16 * J * (NQD * b + kq))
                step_over()
                wait(sp, o_st[j], 16 * J * (NQD * (b - 1) + kq + 1))
                start_load(sp, b, kq, j)

            def store(b, kq, j):
                sp.wait_ge(o_out, NC * b + RING * kq + 2 * j + 2)
                step_over()
                for r in range(J):
                    sp.dma_start(rows(out, b, kq, j)[r],
                                 x1[32 * r:32 * r + 32, bass.ds(4 * GC * kq + 2 * GC * j, 2 * GC), :]
                                 ).then_inc(o_st[j], 16)

            def shift(a, b, kq, slot):
                if not (isinstance(kq, int) and kq == 0 and slot < 3):
                    sp.wait_ge(conv[a], 2 * NC * b + 2 * (RING * kq + slot - RING + 1) + 1)
                    step_over()
                sp.wait_ge(lo_out, 2 * NC * b + NC * a + RING * kq + slot + 1)
                for dst, src in copies(a, slot):
                    sp.dma_start(dst, src).then_inc(mid_in[a][slot], 16)

            def body(b, last=False):
                shift(0, b, 0, 3)
                if not last:
                    wait(sp, inv_ps, IP * (b + 1))
                    load_modes(sp, b + 1)
                for slot in range(RING):
                    shift(0, b, 1, slot)
                    load(b, NQD - 2 + slot // 2, slot % 2)
                with sp.Fori(2, NQD) as kq:
                    for slot in range(RING):
                        shift(0, b, kq, slot)
                sp.wait_ge(conv[0], 2 * NC * b + 2 * (NC - RING + 1))
                sp.dma_start(mid[0][64:96, :, 0:1, :], win[0][96:128, :, GR - 1:GR, :]).then_inc(below[0], 16)
                wait(sp, conv[1], 2 * NC * b)
                sp.dma_start(mid[1][0:64, :, 0:1, :], zeros[0:64]).then_inc(above, 16)
                for slot in range(RING):
                    shift(1, b, 0, slot)
                for slot in range(RING):
                    shift(1, b, 1, slot)
                    if slot % 2:
                        store(b, 0, slot // 2)
                with sp.Fori(2, NQD) as kq:
                    for slot in range(RING):
                        shift(1, b, kq, slot)
                        if slot % 2:
                            if not last:
                                load(b + 1, kq - 2, slot // 2)
                            store(b, kq - 1, slot // 2)
                sp.dma_start(mid[1][64:128, :, 0:1, :], zeros[64:128]).then_inc(below[1], 16)
                if not last:
                    for slot in range(3):
                        shift(0, b + 1, 0, slot)
                for j in range(2):
                    store(b, NQD - 1, j)

            sp.wait_ge(zeroed, 1)
            for slot in range(3):
                shift(0, 0, 0, slot)
            for j in range(2):
                load(0, 1, j)
            peeled(sp, body)
            for i in range(2):
                sp.wait_ge(o_st[i], 16 * J * B * NQD)

        @block.gpsimd
        def _(pool):
            nc.gpsimd.memset(zeros[:], 0.0).then_inc(zeroed, 1)

            def body(b, last=False):
                for n in range(2 * NC):
                    a, k = divmod(n, NC)
                    g0 = GC * k % GR
                    pool.wait_ge(hi_out, 2 * NC * b + n + 1)
                    nc.gpsimd.tensor_tensor(win[a][:, 1, g0:g0 + GC, X0:X0 + W + 1 - a], hn[n % 2][:, :, 0:W + 1 - a],
                                            win[a][:, 0, g0:g0 + GC, X0:X0 + W + 1 - a], ALU.subtract
                                            ).then_inc(lo_out, 1)

            peeled(pool, body)

        @block.scalar
        def _(act):
            def produce(a, b, k):
                n = 2 * NC * b + NC * a + k
                g0 = GC * k % GR
                wait(act, lo_out, n - 1)
                wait(act, conv[a], 2 * NC * b + max(0, 2 * (k - RING + 1)))
                wd = W + 1 - a
                if a == 0:
                    act.wait_ge(x_in[k // 2 % 2], 16 * J * (NQD * b + k // RING + 1))
                    s, t = scc[:, 0:1], scc[:, 1:2]
                    nc.scalar.activation(hn[k % 2][:, :, 0:W], x1[:, GC * k:GC * (k + 1)], ACT.Identity, bias=t, scale=s).then_inc(h_out, 1)
                    nc.scalar.activation(hn[k % 2][:, :, W:W + 1], x1[:, GC * k:GC * (k + 1), W - 1:W], ACT.Identity,
                                         bias=t, scale=s).then_inc(h_out, 1)
                    act.wait_ge(h_out, 3 * NC * b + 2 * k + 2)
                else:
                    nc.scalar.activation(hn[k % 2][:, :, 0:W], x1[:, GC * k:GC * (k + 1)], ACT.Identity,
                                         bias=sc1[:, 1:2], scale=sc1[:, 0:1]).then_inc(h_out, 1)
                    act.wait_ge(h_out, 3 * NC * b + 2 * NC + k + 1)
                nc.scalar.copy(win[a][:, 0, g0:g0 + GC, X0:X0 + wd], hn[k % 2][:, :, 0:wd]).then_inc(hi_out, 1)

            def invert(b, i, slot, halves=(0, 1)):
                act.wait_ge(inv_ps, IP * b + i + 1)
                for h in halves:
                    last = nc.scalar.copy(
                        gi[0:64, :, 8 * i + h:8 * i + 8:2].rearrange("p h o -> p o h"),
                        ps[64 * h:64 * h + 64, 2 * slot:2 * slot + 2].rearrange("p a (c h) -> p (a c) h", c=2))
                if h:
                    last.then_inc(inv_hi, 1)

            def body(b, last=False):
                nc.scalar.copy(scc[:], sc0[:, b:b + 1, :] if isinstance(b, int) else sc0[:, bass.ds(b, 1), :]).then_inc(scc_out, 1)
                act.wait_ge(scc_out, b + 1)
                for k in range(NC):
                    produce(0, b, k)
                if not last:
                    invert(b + 1, 0, (IP + NC) % NP)
                    invert(b + 1, 1, (IP + NC + 1) % NP, halves=(0,))
                act.wait_ge(mean_out, 2 * b + 2)
                nc.scalar.activation(sd[:], ps_s[:, 1:2], ACT.Sqrt, bias=eps[:, 0:1], scale=SH ** -2).then_inc(std_out, 1)
                if not last:
                    invert(b + 1, 1, (IP + NC + 1) % NP, halves=(1,))
                act.wait_ge(norm_out, b + 1)
                for k in range(NC):
                    produce(1, b, k)
                    if not last and 2 <= k + 1 < IP:
                        invert(b + 1, k + 1, (IP + NC + k + 1) % NP)

            for i in range(IP):
                invert(0, i, i % NP)
            peeled(act, body)

        LINKS = 9

        @block.vector
        def _(dve):
            def invert(b, i, slot, halves=(0, 1)):
                dve.wait_ge(inv_hi, IP * b + i + 1)
                for h in halves:
                    last = nc.vector.tensor_tensor(
                        gi[64:128, :, 8 * i + h:8 * i + 8:2].rearrange("p h o -> p o h"),
                        ps[64 * h:64 * h + 64, 2 * slot:2 * slot + 2].rearrange("p a (c h) -> p (a c) h", c=2),
                        gi[0:64, :, 8 * i + h:8 * i + 8:2].rearrange("p h o -> p o h"), ALU.subtract)
                if h:
                    last.then_inc(inv_lo, 1)

            def constant_mode(b):
                dve.wait_ge(gm_in, 32 * b + 32)
                nc.vector.tensor_tensor(gm[0:1, 0, :], gm[0:1, 0, :], dc[:], ALU.add).then_inc(gm_dc, 1)

            def evacuate(a, b, k):
                i = IP + (NC + IP) * a + k
                slot = i % NP
                dve.wait_ge(conv[a], 2 * NC * b + 2 * k + 2)
                banks = ps[:, 2 * slot:2 * slot + 2, :].rearrange("p a w -> p (a w)")
                if a == 0:
                    nc.vector.scalar_tensor_tensor(
                        out=x1[:, GC * k:GC * (k + 1)].rearrange("p g w -> p (g w)"), in0=banks, scalar=q[:, 0:1],
                        in1=x1[:, GC * k:GC * (k + 1)].rearrange("p g w -> p (g w)"), op0=ALU.mult, op1=ALU.add).then_inc(x1_out, 1)
                    dve.wait_ge(x1_out, NC * b + k + 1)
                    for h in range(2):
                        last = nc.vector.bn_stats(bs[:, 2 * k + h, :],
                                                  x1[:, GC * k + 2 * h:GC * k + 2 * h + 2].rearrange("p g w -> p (g w)"))
                    last.then_inc(bn_out, 1)
                else:
                    nc.vector.scalar_tensor_tensor(
                        out=x1[:, GC * k:GC * (k + 1)].rearrange("p g w -> p (g w)"), in0=banks, scalar=q[:, 1:2],
                        in1=x1[:, GC * k:GC * (k + 1)].rearrange("p g w -> p (g w)"), op0=ALU.mult, op1=ALU.add
                        ).then_inc(o_out, 1)

            def statistics(b, meanwhile):
                m = LINKS * b
                dve.wait_ge(bn_out, NC * b + NC)
                nc.vector.tensor_copy(pad[:], bs[:, 0, 0:1])
                nc.vector.bn_aggr(mv[:], bs[:].rearrange("p n s -> p (n s)")).then_inc(own, 1)
                dve.wait_ge(own, m + 1)
                nc.vector.tensor_tensor(mc[:], mv[:, 0:1], b3p[:], ALU.subtract).then_inc(mean_in, 1)
                dve.wait_ge(mean_in, 2 * b + 1)
                dve.wait_ge(mean_out, 2 * b + 1)
                nc.vector.tensor_tensor(dm[:], mc[:], ps_s[:, 0:1], ALU.subtract).then_inc(own, 1)
                dve.wait_ge(own, m + 2)
                nc.vector.scalar_tensor_tensor(out=vv[:], in0=dm[:], scalar=dm[:, 0:1], in1=mv[:, 1:2],
                                               op0=ALU.mult, op1=ALU.add).then_inc(mean_in, 1)
                meanwhile()
                dve.wait_ge(std_out, b + 1)
                nc.vector.tensor_scalar(hv[:], ps_s[:, 1:2], 0.5 / SH ** 2, 0.5 * EPS / SH ** 2, ALU.mult, ALU.add
                                        ).then_inc(own, 1)
                nc.vector.reciprocal(rs[:], sd[:]).then_inc(own, 1)
                nc.vector.tensor_tensor(ns[:], b3p[:], ps_s[:, 0:1], ALU.add).then_inc(own, 1)
                dve.wait_ge(own, m + 5)
                nc.vector.tensor_scalar(dm[:], ns[:], -1.0, None, ALU.mult).then_inc(own, 1)
                nc.vector.tensor_tensor(hv[:], hv[:], rs[:], ALU.mult).then_inc(own, 1)
                dve.wait_ge(own, m + 7)
                nc.vector.scalar_tensor_tensor(out=rs[:], in0=sd[:], scalar=0.5, in1=hv[:], op0=ALU.mult, op1=ALU.add
                                               ).then_inc(own, 1)
                dve.wait_ge(own, m + 8)
                nc.vector.reciprocal(sc1[:, 0:1], rs[:]).then_inc(own, 1)
                dve.wait_ge(own, m + 9)
                nc.vector.tensor_tensor(sc1[:, 1:2], dm[:], sc1[:, 0:1], ALU.mult).then_inc(norm_out, 1)

            def body(b, last=False):
                for k in range(NC):
                    evacuate(0, b, k)
                    if k == 0 and not last:
                        constant_mode(b + 1)
                def first_half():
                    if not last:
                        invert(b + 1, 0, (IP + NC) % NP, halves=(0,))

                statistics(b, first_half)
                if not last:
                    for i in range(IP):
                        invert(b + 1, i, (IP + NC + i) % NP, halves=(0, 1) if i else (1,))
                for k in range(NC):
                    evacuate(1, b, k)

            constant_mode(0)
            for i in range(IP):
                invert(0, i, i % NP)
            peeled(dve, body)

        @block.tensor
        def _(pe):
            def moving(a, buf, hl, g, dx):
                g %= GR
                c = slice(X0 + dx, X0 + dx + W)
                if g + 2 <= GR:
                    return [(0, 2, buf[a][:, hl, g:g + 2, c])]
                return [(0, 1, buf[a][:, hl, g:g + 1, c]), (1, 1, buf[a][:, hl, 0:1, c])]

            def chunk_ready(a, b, k):
                if k < NC:
                    pe.wait_ge(mid_in[a][k % RING], mid_count(a, b, k // RING, k % RING))
                else:
                    pe.wait_ge(below[a], 16 * (b + 1))
                if a == 1 and k == 0:
                    pe.wait_ge(above, 16 * (b + 1))

            def layer0(b, p):
                k = p // 2
                bank = bank_of(IP + k) + p % 2
                if p % 2 == 0:
                    chunk_ready(0, b, k)
                    if k >= NP:
                        pe.wait_ge(x1_out, NC * b + k - NP + 1)
                    elif isinstance(b, int) and b == 0:
                        pe.wait_ge(inv_lo, IP - NP + k + 1)
                    else:
                        pe.wait_ge(o_out, NC * b + k - NP + 1)
                else:
                    chunk_ready(0, b, k + 1)
                if p == 0:
                    pe.wait_ge(inv_lo, IP * (b + 1))
                g = 2 * p
                for wl, xl in ((0, 0), (1, 0), (0, 1)):
                    for half, buf, gg in ((0, win, g), (1, mid, g + 1)):
                        for at, count, rhs in moving(0, buf, xl, gg, 0):
                            nc.tensor.matmul(ps[64 * half:64 * half + 64, bank, W * at:W * (at + count)],
                                             lw0[:, wl].rearrange("p m o -> p (m o)"), rhs,
                                             start=(wl == xl == at == 0), stop=False, skip_group_check=True)
                for wl, xl in ((0, 0), (1, 0), (0, 1)):
                    for at, count, rhs in moving(0, win, xl, g, 1):
                        nc.tensor.matmul(ps[:, bank, W * at:W * (at + count)],
                                         lwr[:, wl].rearrange("p m o -> p (m o)"), rhs,
                                         start=False, stop=False, skip_group_check=True)
                for i in range(2):
                    for hl in range(2):
                        r = J * (g + i)
                        last = nc.tensor.matmul(ps[:, bank, W * i:W * (i + 1)],
                                                gi[:, r:r + J, :].rearrange("p h o -> p (h o)"), iw[:, hl, :],
                                                start=False, stop=(i == hl == 1), skip_group_check=True)
                last.then_inc(conv[0], 1)

            def layer1(b, p, last_image):
                k = p // 2
                bank = bank_of(2 * IP + NC + k) + p % 2
                if p % 2 == 0:
                    chunk_ready(1, b, k)
                    if k >= NP:
                        pe.wait_ge(o_out, NC * b + k - NP + 1)
                    elif last_image:
                        pe.wait_ge(x1_out, NC * b + NC)
                    else:
                        pe.wait_ge(inv_lo, IP * (b + 1) + IP - NP + k + 1)
                else:
                    chunk_ready(1, b, k + 1)
                g = 2 * p
                for dx in range(3):
                    for wl, xl in ((0, 0), (1, 0), (0, 1)):
                        for j, variant, buf, gg in ((0, 0, mid, g), (1, 1, win, g), (2, 0, win, g), (3, 1, mid, g + 1)):
                            for at, count, rhs in moving(1, buf, xl, gg, dx - 1):
                                last = nc.tensor.matmul(ps[32 * j:32 * j + 32, bank, W * at:W * (at + count)],
                                                        lw1[:, wl, variant, dx, :], rhs,
                                                        start=(dx == wl == xl == at == 0),
                                                        stop=(dx == 2 and xl == 1), skip_group_check=True)
                last.then_inc(conv[1], 1)

            def bank_of(i):
                return 2 * (i % NP)

            def invert(b, i, bank):
                if i == 0:
                    pe.wait_ge(gm_dc, b + 1)
                if i >= NP:
                    pe.wait_ge(inv_lo, IP * b + i - NP + 1)
                elif not (isinstance(b, int) and b == 0):
                    pe.wait_ge(x1_out, NC * b - NP + i + 1)
                for bk in range(2):
                    for c in range(2):
                        for t in range(4):
                            o = 8 * i + 4 * bk + 2 * c + t // 2
                            last = nc.tensor.matmul(
                                ps[32 * t:32 * t + 32, bank + bk, H * c:H * (c + 1)],
                                gm[:, :, o], ih[:, t % 2, :], start=(c == 0), stop=(c == 1), skip_group_check=True)
                last.then_inc(inv_ps, 1)

            def body(b, last=False):
                for p in range(2 * NC):
                    layer0(b, p)
                def inverts(which):
                    for i in () if last else which:
                        invert(b + 1, i, bank_of(IP + NC + i))

                inverts((0, 1))
                for i in range(2):
                    pe.wait_ge(mean_in, 2 * b + i + 1)
                    nc.tensor.matmul(ps_s[:, i:i + 1], mats[:, 0, :], (mc, vv)[i][:], start=True, stop=True
                                     ).then_inc(mean_out, 1)
                inverts((2, 3))
                for p in range(2 * NC):
                    layer1(b, p, last)

            for i in range(IP):
                invert(0, i, bank_of(i))
            peeled(pe, body)


def setup(nc, cw, cb, w3, b3, t_inv_h, t_inv_w, mats, gmax, stat_d, win, mid, ih, iw, lw0, lwr, lw1,
          sc0, eps, b3p, dc, q, ps_s, first_loads):
    with ExitStack() as ctx:
        def sb(name, shape, dt):
            return ctx.enter_context(nc.sbuf_tensor(f"su_{name}", shape, dt))

        def sem(name):
            return ctx.enter_context(nc.semaphore(f"su_{name}"))

        c0 = sb("c0", [P, 3, C], F32)
        c1 = sb("c1", [P, C, 9], F32)
        t0 = sb("t0", [P, 3, C], F32)
        z = sb("z", [P, 3 * C], F32)
        h0 = sb("h0", [P, 2, 3, C], F16)
        h1 = sb("h1", [P, 2, 9, C], F16)
        fw = sb("fw", [P, W], F32)
        mx = sb("mx", [P, 3], F32)
        mq = sb("mq", [P, 3], F32)
        iq = sb("iq", [P, 3], F32)
        row = sb("row", [1, 8], F32)
        cbr = sb("cbr", [1, 3, C], F32)
        ones = sb("ones", [1, P], F32)
        LOADS = 16 * (6 * J + 4)
        loaded = sem("loaded")
        own = sem("own_setup")
        max_ps = sem("max_ps")
        max_row = sem("max_row")
        cleared = sem("cleared")
        block = ctx.enter_context(nc.Block())

        @block.sync
        def _(sp):
            n = 0
            with nc.allow_non_contiguous_dma("weights are gathered once"):
                for j in range(J):
                    s = slice(32 * j, 32 * j + 32)
                    for t in range(3):
                        sp.dma_start(c0[s, t, :], cw[:, C * t:C * (t + 1)].rearrange("o c -> c o")).then_inc(loaded, 16)
                    sp.dma_start(c1[s], w3.rearrange("o c y x -> c o (y x)")).then_inc(loaded, 16)
                    sp.dma_start(sc0[s], stat_d.rearrange("b t c -> c b t")).then_inc(loaded, 16)
                    sp.dma_start(b3p[s], b3.rearrange("(c u) -> c u", u=1)).then_inc(loaded, 16)
                    n += 6
            sp.dma_start(ih[:], t_inv_h).then_inc(loaded, 16)
            sp.dma_start(fw[:], t_inv_w).then_inc(loaded, 16)
            sp.dma_start(cbr[:, 0, :], cb.rearrange("(u c) -> u c", u=1)).then_inc(loaded, 16)
            sp.dma_start(cbr[:, 1, :], b3.rearrange("(u c) -> u c", u=1)).then_inc(loaded, 16)
            assert 16 * (n + 4) == LOADS
            first_loads(sp)
            sp.wait_ge(loaded, LOADS)

        @block.gpsimd
        def _(pool):
            for t in (*win, *mid):
                last = nc.gpsimd.memset(t[:].rearrange("p a g w -> p (a g w)"), 0.0)
                last.then_inc(cleared, 1)

        @block.tensor
        def _(pe):
            pe.wait_ge(max_row, 1)
            for i in range(3):
                nc.tensor.matmul(ps_s[0:1, P * i:P * (i + 1)], mx[:, i:i + 1], mats[:, 2, :], start=True, stop=True
                                 ).then_inc(max_ps, 1)
            pe.wait_ge(max_row, 2)
            nc.tensor.matmul(ps_s[:, 384:387], ones[0:1, :], row[0:1, 0:3], start=True, stop=True).then_inc(max_ps, 1)

        @block.vector
        def _(dve):
            count = [0]

            def link(ins):
                count[0] += 1
                ins.then_inc(own, 1)
                dve.wait_ge(own, count[0])

            V = nc.vector
            V.memset(eps[:], EPS / SH ** 2)
            V.memset(ones[:], 1.0)
            V.memset(lw0[:].rearrange("p a b c -> p (a b c)"), 0.0)
            V.memset(lwr[:].rearrange("p a b c -> p (a b c)"), 0.0)
            V.memset(lw1[:].rearrange("p a b c d -> p (a b c d)"), 0.0)
            dve.wait_ge(loaded, LOADS)
            link(V.tensor_tensor(cbr[:, 2, :], cbr[:, 0, :], cbr[:, 1, :], ALU.add))
            link(V.tensor_scalar(dc[:], cbr[:, 2, :], float(H * W), None, ALU.mult))
            link(V.tensor_tensor(z[:, 0:C], c0[:, 0, :], c0[:, 1, :], ALU.subtract))
            link(V.tensor_tensor(t0[:, 0, :], z[:, 0:C], c0[:, 2, :], ALU.subtract))
            link(V.tensor_copy(t0[:, 1:3, :], c0[:, 1:3, :]))
            link(V.memset(mx[:], 0.0))
            link(V.tensor_reduce(mx[0:1, 2:3], cbr[:, 2, :], AX_X, ALU.max, apply_absolute_value=True))
            link(V.scalar_tensor_tensor(out=mx[:, 2:3], in0=gmax[:], scalar=128.0 / (H * W), in1=mx[:, 2:3],
                                        op0=ALU.mult, op1=ALU.add))
            link(V.tensor_reduce(mx[:, 0:1], t0[:].rearrange("p t o -> p (t o)"), AX_X, ALU.max, apply_absolute_value=True))
            link(V.tensor_reduce(mx[:, 1:2], c1[:].rearrange("p o t -> p (o t)"), AX_X, ALU.max, apply_absolute_value=True))
            V.tensor_scalar(mx[:], mx[:], 1e-30, None, ALU.max).then_inc(max_row, 1)
            dve.wait_ge(max_ps, 3)
            link(V.tensor_reduce(row[:, 4:7], ps_s[0:1, 0:3 * P].rearrange("p (a b) -> p a b", a=3), AX_X, ALU.max))
            V.tensor_copy(row[:, 0:3], row[:, 4:7]).then_inc(max_row, 1)
            dve.wait_ge(max_ps, 4)
            link(V.tensor_copy(mq[:], ps_s[:, 384:387]))
            link(V.tensor_scalar(q[:, 2:3], mq[:, 2:3], 1.0 / 128, None, ALU.mult))
            link(V.tensor_tensor(mq[:, 0:1], mq[:, 0:1], q[:, 2:3], ALU.max))
            link(V.tensor_scalar(q[:, 0:2], mq[:, 0:2], 1.0 / (SW * SH), None, ALU.mult))
            link(V.reciprocal(iq[:], mq[:]))
            link(V.tensor_scalar(iq[:], iq[:], SW, None, ALU.mult))
            link(V.tensor_tensor(q[:, 3:4], mq[:, 2:3], iq[:, 0:1], ALU.mult))
            link(V.tensor_scalar(q[:, 3:4], q[:, 3:4], SH / SW, None, ALU.mult))
            link(V.tensor_scalar(ih[:], ih[:], iq[:, 2:3], None, ALU.mult))
            link(V.tensor_scalar(t0[:], t0[:], iq[:, 0:1], None, ALU.mult))
            link(V.tensor_scalar(c1[:], c1[:], iq[:, 1:2], None, ALU.mult))
            link(V.tensor_scalar(fw[:], fw[:], q[:, 3:4], None, ALU.mult))
            link(V.tensor_copy(iw[:, 0, :], fw[:]))
            link(V.tensor_tensor(iw[:, 1, :], fw[:], iw[:, 0, :], ALU.subtract))
            link(V.tensor_copy(h0[:, 0], t0[:]))
            link(V.tensor_tensor(h0[:, 1], t0[:], h0[:, 0], ALU.subtract))
            link(V.tensor_copy(h1[:, 0], c1[:].rearrange("p o t -> p t o")))
            link(V.tensor_tensor(h1[:, 1], c1[:].rearrange("p o t -> p t o"), h1[:, 0], ALU.subtract))
            for m in range(2):
                for blk, tap in ((m, 0), (m + 1, 1)):
                    s = slice(32 * blk, 32 * blk + 32)
                    link(V.tensor_copy(lw0[s, :, m, :], h0[s, :, tap, :]))
            for j in range(J):
                s = slice(32 * j, 32 * j + 32)
                link(V.tensor_copy(lwr[s, :, j, :], h0[s, :, 2, :]))
            for variant in range(2):
                for dy in range(3):
                    s = slice(32 * (dy + 1 - variant), 32 * (dy + 2 - variant))
                    link(V.tensor_copy(lw1[s, :, variant, :, :], h1[s, :, 3 * dy:3 * dy + 3, :]))


_INS = ["x", "L0_conv_conv_w", "L0_conv_conv_b", "L0_conv_w1r", "L0_conv_w1i", "L0_conv_w2r", "L0_conv_w2i",
        "L1_conv_weight", "L1_conv_bias"]


def kernel(**inputs):
    import numpy as _np
    import concourse.bacc as _bacc
    from concourse import mybir as _mybir
    from concourse.bass_utils import run_bass_kernel_spmd as _run

    nc = _bacc.Bacc("TRN2", target_bir_lowering=False, num_devices=1)
    arrays, args = {}, []
    data = {name: inputs[name] for name in _INS}
    data.update(tables())
    for name, a in data.items():
        a = _np.ascontiguousarray(a)
        arrays[f"in_{name}_dram"] = a
        args.append(nc.dram_tensor(f"in_{name}_dram", a.shape, _mybir.dt.from_np(a.dtype), kind="ExternalInput").ap())
    args.append(nc.dram_tensor("out_0_dram", (B, C, H, W), _mybir.dt.float32, kind="ExternalOutput").ap())
    program(nc, *args)
    r = _run(nc, [arrays], core_ids=[0])
    return r.results[0]["out_0_dram"]
```
